# Optimizing a Trainium2 kernel written in Bass

```python
import numpy as np
import jax
import jax.numpy as jnp

def _softmax(x, axis=-1):
    return jax.nn.softmax(x, axis=axis)

def _gelu(x):
    return jax.nn.gelu(x, approximate=True)

def _silu(x):
    return jax.nn.silu(x)

def _sigmoid(x):
    return jax.nn.sigmoid(x)

def _layernorm(x, axis=-1, eps=1e-05):
    m = jnp.mean(x, axis=axis, keepdims=True)
    v = jnp.var(x, axis=axis, keepdims=True)
    return (x - m) / jnp.sqrt(v + eps)

def _scatter_add(tgt, idx, src, axis=0):
    return tgt.at[idx].add(src)

def _segment_sum(src, seg, n):
    return jax.ops.segment_sum(src, seg, n)
kernel_name = 'mk_xattn_ffn_d1_seqx_r4_fa1626'

def setup_inputs(seed: int=0):
    np.random.seed(seed)
    _w = jnp.asarray

    def _rec_inputs():
        import jax
        import jax.numpy as jnp
        _rk = jax.random.key(seed)
        x = -0.0005146 + 1 * jax.random.normal(jax.random.fold_in(_rk, 1), (16, 256, 256), jnp.float32)
        _lenS = 256 - jax.random.randint(jax.random.fold_in(_rk, 7), (16,), 0, max(1, 256 // 4) + 1, jnp.int32)
        _lenS2 = 256 - jax.random.randint(jax.random.fold_in(_rk, 8), (16,), 0, max(1, 256 // 4) + 1, jnp.int32)
        _ctx_768P = jax.random.normal(jax.random.fold_in(_rk, 11), (16, 16, 192), jnp.float32)
        _ctx_768c = jax.random.dirichlet(jax.random.fold_in(_rk, 511), 0.3 * jnp.ones((16,), jnp.float32), (16, 256))
        _ctx_768t = jnp.einsum('bsk,bkd->bsd', _ctx_768c, _ctx_768P)
        _ctx_768t = _ctx_768t * jax.lax.rsqrt(jnp.mean(jnp.square(_ctx_768t)) + 1e-12) * 0.953939
        ctx_768 = -0.00040386 + 0.999972 * (_ctx_768t + 0.3 * jax.random.normal(jax.random.fold_in(_rk, 611), (16, 256, 192), jnp.float32))
        _validS = jnp.arange(256)[None, :] < _lenS[:, None]
        _validS2 = jnp.arange(256)[None, :] < _lenS2[:, None]
        _causal = jnp.tril(jnp.ones((256, 256), dtype=bool))
        mask_BxS2_bk0 = jnp.logical_not(jnp.broadcast_to(_validS2[:, :], (16, 256)))
        return (x, ctx_768, mask_BxS2_bk0)
    x, ctx_768, mask_BxS2_bk0 = _rec_inputs()

    def _L0_xattn_setup():
        import jax, jax.numpy as jnp
        import numpy as np
        DIM_IN, DIM_LAT, DIM_HEAD = (192, 256, 64)
        INNER = max(DIM_LAT, DIM_IN)
        HEADS = INNER // DIM_HEAD
        SCALE = DIM_HEAD ** (-0.5)
        RMS_EPS = 1e-08
        LN_EPS = 1e-05

        def layernorm(x, g, b):
            mu = jnp.mean(x, axis=-1, keepdims=True)
            var = jnp.mean((x - mu) ** 2, axis=-1, keepdims=True)
            return (x - mu) * jax.lax.rsqrt(var + LN_EPS) * g + b

        def rmsnorm(x, gamma):
            norm = jnp.sqrt(jnp.sum(x * x, axis=-1, keepdims=True)) * x.shape[-1] ** (-0.5)
            return x / jnp.maximum(norm, RMS_EPS) * gamma
        key = jax.random.key(seed)
        ks = jax.random.split(key, 12)
        b, n, m = (4, 1024, 128)
        x = jax.random.normal(ks[0], (b, n, DIM_IN), jnp.float32)
        latents = jax.random.normal(ks[1], (b, m, DIM_LAT), jnp.float32)
        mask = jax.random.randint(ks[2], (b, n), 0, 2).astype(bool)
        s = lambda k, sh, fan: jax.random.normal(k, sh, jnp.float32) * fan ** (-0.5)
        return {'x': x, 'latents': latents, 'mask': mask, 'ln_x_g': jnp.ones((DIM_IN,), jnp.float32), 'ln_x_b': jnp.zeros((DIM_IN,), jnp.float32), 'ln_l_g': jnp.ones((DIM_LAT,), jnp.float32), 'ln_l_b': jnp.zeros((DIM_LAT,), jnp.float32), 'qn_g': jnp.ones((DIM_HEAD,), jnp.float32), 'kn_g': jnp.ones((DIM_HEAD,), jnp.float32), 'Wq': s(ks[3], (INNER, DIM_LAT), DIM_LAT), 'Wkv': s(ks[4], (2 * INNER, DIM_IN), DIM_IN), 'Wlkv': s(ks[5], (2 * INNER, DIM_LAT), DIM_LAT), 'Wo': s(ks[6], (DIM_LAT, INNER), INNER), 'bo': jnp.zeros((DIM_LAT,), jnp.float32)}
    _L0_xattn_all = _L0_xattn_setup()
    _L0_xattn_in = {k: v for k, v in _L0_xattn_all.items() if k in ('ln_x_g', 'ln_x_b', 'ln_l_g', 'ln_l_b', 'qn_g', 'kn_g', 'Wq', 'Wkv', 'Wlkv', 'Wo', 'bo')}
    del _L0_xattn_all

    def _L0_ffn_setup():
        import jax, jax.numpy as jnp
        import numpy as np
        DIM = 256
        NUM_HEAVY = 256
        N_ITERS = 50
        EPS = 1.0
        FETCH_K_RATIO = 9.0 / 8.0

        def rms_norm(x, gamma):
            norm = jnp.maximum(jnp.linalg.norm(x, axis=-1, keepdims=True), 1e-12)
            return x / norm * x.shape[-1] ** 0.5 * gamma

        def feed_forward(x, gamma, w1, b1, w2, b2):
            h = jax.nn.gelu(rms_norm(x, gamma) @ w1 + b1, approximate=False)
            return h @ w2 + b2

        def coor_descent(s, k, n_iters, eps):
            logk = jnp.log(jnp.asarray(k, dtype=s.dtype))

            def step(ab, _):
                a, b = ab
                sb = (s + b) / eps
                a = eps * (logk - jax.scipy.special.logsumexp(sb, axis=-1, keepdims=True))
                b = -jax.nn.relu(s + a)
                return ((a, b), None)
            a0 = jnp.zeros_like(s[..., :1])
            b0 = -s
            (a, b), _ = jax.lax.scan(step, (a0, b0), None, length=n_iters)
            return jnp.exp((s + a + b) / eps)
        key = jax.random.key(seed)
        ks = jax.random.split(key, 8)
        b, n, d = (4, 2048, DIM)
        dl, dh = (int(d * 0.5), d * 4)
        u = lambda k, shape, fan_in: jax.random.uniform(k, shape, jnp.float32, -1.0, 1.0) / np.sqrt(fan_in)
        return {'x': jax.random.normal(ks[0], (b, n, d), jnp.float32), 'routing_token': jax.random.normal(ks[1], (d,), jnp.float32), 'light_gamma': jnp.ones((d,), jnp.float32), 'light_w1': u(ks[2], (d, dl), d), 'light_b1': jnp.zeros((dl,), jnp.float32), 'light_w2': u(ks[3], (dl, d), dl), 'light_b2': jnp.zeros((d,), jnp.float32), 'heavy_gamma': jnp.ones((d,), jnp.float32), 'heavy_w1': u(ks[4], (d, dh), d), 'heavy_b1': jnp.zeros((dh,), jnp.float32), 'heavy_w2': u(ks[5], (dh, d), dh), 'heavy_b2': jnp.zeros((d,), jnp.float32)}
    _L0_ffn_all = _L0_ffn_setup()
    _L0_ffn_in = {k: v for k, v in _L0_ffn_all.items() if k in ('routing_token', 'light_gamma', 'light_w1', 'light_b1', 'light_w2', 'light_b2', 'heavy_gamma', 'heavy_w1', 'heavy_b1', 'heavy_w2', 'heavy_b2')}
    del _L0_ffn_all
    return {'x': x, 'ctx_768': ctx_768, 'mask_BxS2_bk0': mask_BxS2_bk0, 'L0_xattn_ln_x_g': _L0_xattn_in['ln_x_g'], 'L0_xattn_ln_x_b': _L0_xattn_in['ln_x_b'], 'L0_xattn_ln_l_g': _L0_xattn_in['ln_l_g'], 'L0_xattn_ln_l_b': _L0_xattn_in['ln_l_b'], 'L0_xattn_qn_g': _L0_xattn_in['qn_g'], 'L0_xattn_kn_g': _L0_xattn_in['kn_g'], 'L0_xattn_Wq': _L0_xattn_in['Wq'], 'L0_xattn_Wkv': _L0_xattn_in['Wkv'], 'L0_xattn_Wlkv': _L0_xattn_in['Wlkv'], 'L0_xattn_Wo': _L0_xattn_in['Wo'], 'L0_xattn_bo': _L0_xattn_in['bo'], 'L0_ffn_routing_token': _L0_ffn_in['routing_token'], 'L0_ffn_light_gamma': _L0_ffn_in['light_gamma'], 'L0_ffn_light_w1': _L0_ffn_in['light_w1'], 'L0_ffn_light_b1': _L0_ffn_in['light_b1'], 'L0_ffn_light_w2': _L0_ffn_in['light_w2'], 'L0_ffn_light_b2': _L0_ffn_in['light_b2'], 'L0_ffn_heavy_gamma': _L0_ffn_in['heavy_gamma'], 'L0_ffn_heavy_w1': _L0_ffn_in['heavy_w1'], 'L0_ffn_heavy_b1': _L0_ffn_in['heavy_b1'], 'L0_ffn_heavy_w2': _L0_ffn_in['heavy_w2'], 'L0_ffn_heavy_b2': _L0_ffn_in['heavy_b2']}

def reference(x, ctx_768, mask_BxS2_bk0, L0_xattn_ln_x_g, L0_xattn_ln_x_b, L0_xattn_ln_l_g, L0_xattn_ln_l_b, L0_xattn_qn_g, L0_xattn_kn_g, L0_xattn_Wq, L0_xattn_Wkv, L0_xattn_Wlkv, L0_xattn_Wo, L0_xattn_bo, L0_ffn_routing_token, L0_ffn_light_gamma, L0_ffn_light_w1, L0_ffn_light_b1, L0_ffn_light_w2, L0_ffn_light_b2, L0_ffn_heavy_gamma, L0_ffn_heavy_w1, L0_ffn_heavy_b1, L0_ffn_heavy_w2, L0_ffn_heavy_b2):
    import jax
    import jax.numpy as jnp

    def _L0_xattn_ref(x, latents, mask, ln_x_g, ln_x_b, ln_l_g, ln_l_b, qn_g, kn_g, Wq, Wkv, Wlkv, Wo, bo):
        import jax, jax.numpy as jnp
        import numpy as np
        DIM_IN, DIM_LAT, DIM_HEAD = (192, 256, 64)
        INNER = max(DIM_LAT, DIM_IN)
        HEADS = INNER // DIM_HEAD
        SCALE = DIM_HEAD ** (-0.5)
        RMS_EPS = 1e-08
        LN_EPS = 1e-05

        def layernorm(x, g, b):
            mu = jnp.mean(x, axis=-1, keepdims=True)
            var = jnp.mean((x - mu) ** 2, axis=-1, keepdims=True)
            return (x - mu) * jax.lax.rsqrt(var + LN_EPS) * g + b

        def rmsnorm(x, gamma):
            norm = jnp.sqrt(jnp.sum(x * x, axis=-1, keepdims=True)) * x.shape[-1] ** (-0.5)
            return x / jnp.maximum(norm, RMS_EPS) * gamma
        b, n, _ = x.shape
        m = latents.shape[1]
        xn = layernorm(x, ln_x_g, ln_x_b)
        ln = layernorm(latents, ln_l_g, ln_l_b)
        q = ln @ Wq.T
        kv = jnp.concatenate([xn @ Wkv.T, ln @ Wlkv.T], axis=1)
        k, v = (kv[..., :INNER], kv[..., INNER:])
        split_heads = lambda t: t.reshape(t.shape[0], t.shape[1], HEADS, DIM_HEAD).transpose(0, 2, 1, 3)
        q, k, v = (split_heads(q), split_heads(k), split_heads(v))
        qn = rmsnorm(q, qn_g) * SCALE
        kn = rmsnorm(k, kn_g)
        attn = jnp.einsum('bhid,bhjd->bhij', qn, kn)
        full_mask = jnp.pad(mask, ((0, 0), (0, m)), constant_values=True)
        attn = jnp.where(full_mask[:, None, None, :], attn, -jnp.finfo(attn.dtype).max)
        attn = jax.nn.softmax(attn, axis=-1)
        out = jnp.einsum('bhij,bhjd->bhid', attn, v)
        out = out.transpose(0, 2, 1, 3).reshape(b, m, INNER)
        return out @ Wo.T + bo

    def _L0_ffn_ref(x, routing_token, light_gamma, light_w1, light_b1, light_w2, light_b2, heavy_gamma, heavy_w1, heavy_b1, heavy_w2, heavy_b2):
        import jax, jax.numpy as jnp
        import numpy as np
        DIM = 256
        NUM_HEAVY = 256
        N_ITERS = 50
        EPS = 1.0
        FETCH_K_RATIO = 9.0 / 8.0

        def rms_norm(x, gamma):
            norm = jnp.maximum(jnp.linalg.norm(x, axis=-1, keepdims=True), 1e-12)
            return x / norm * x.shape[-1] ** 0.5 * gamma

        def feed_forward(x, gamma, w1, b1, w2, b2):
            h = jax.nn.gelu(rms_norm(x, gamma) @ w1 + b1, approximate=False)
            return h @ w2 + b2

        def coor_descent(s, k, n_iters, eps):
            logk = jnp.log(jnp.asarray(k, dtype=s.dtype))

            def step(ab, _):
                a, b = ab
                sb = (s + b) / eps
                a = eps * (logk - jax.scipy.special.logsumexp(sb, axis=-1, keepdims=True))
                b = -jax.nn.relu(s + a)
                return ((a, b), None)
            a0 = jnp.zeros_like(s[..., :1])
            b0 = -s
            (a, b), _ = jax.lax.scan(step, (a0, b0), None, length=n_iters)
            return jnp.exp((s + a + b) / eps)
        b, n, d = x.shape
        light_out = feed_forward(x, light_gamma, light_w1, light_b1, light_w2, light_b2)
        s = jnp.einsum('bnd,d->bn', x, routing_token)
        effective_k = min(NUM_HEAVY * FETCH_K_RATIO, n)
        scores = coor_descent(s, effective_k, N_ITERS, EPS)
        sel_scores, sel_idx = jax.lax.top_k(scores, NUM_HEAVY)
        sel_scores = sel_scores + jax.lax.stop_gradient(1.0 - sel_scores)
        routed = jnp.take_along_axis(x, sel_idx[..., None], axis=1)
        routed_out = feed_forward(routed, heavy_gamma, heavy_w1, heavy_b1, heavy_w2, heavy_b2)
        routed_out = routed_out * sel_scores[..., None]
        batch_idx = jnp.arange(b)[:, None]
        heavy_out = jnp.zeros_like(x).at[batch_idx, sel_idx].set(routed_out)
        return light_out + heavy_out
    x = x + _L0_xattn_ref(ctx_768, _layernorm(x, axis=-1), mask_BxS2_bk0, L0_xattn_ln_x_g, L0_xattn_ln_x_b, L0_xattn_ln_l_g, L0_xattn_ln_l_b, L0_xattn_qn_g, L0_xattn_kn_g, L0_xattn_Wq, L0_xattn_Wkv, L0_xattn_Wlkv, L0_xattn_Wo, L0_xattn_bo)
    x = x + _L0_ffn_ref(_layernorm(x, axis=-1), L0_ffn_routing_token, L0_ffn_light_gamma, L0_ffn_light_w1, L0_ffn_light_b1, L0_ffn_light_w2, L0_ffn_light_b2, L0_ffn_heavy_gamma, L0_ffn_heavy_w1, L0_ffn_heavy_b1, L0_ffn_heavy_w2, L0_ffn_heavy_b2)
    return x

_drawn_inputs = setup_inputs


def setup_inputs(seed=0):
    import zlib

    import numpy as np

    out = dict(_drawn_inputs(seed))
    spreads = {'L0_xattn_ln_x_g': (1.0, 0.6),
     'L0_xattn_ln_x_b': (0.0, 0.515),
     'L0_xattn_ln_l_g': (1.0, 0.2),
     'L0_xattn_ln_l_b': (0.0, 0.1),
     'L0_xattn_qn_g': (1.0, 0.6),
     'L0_xattn_kn_g': (1.0, 0.6),
     'L0_xattn_bo': (0.0, 0.1),
     'L0_ffn_light_gamma': (1.0, 0.2),
     'L0_ffn_light_b1': (0.0, 0.1),
     'L0_ffn_light_b2': (0.0, 0.1),
     'L0_ffn_heavy_gamma': (1.0, 0.2),
     'L0_ffn_heavy_b1': (0.0, 0.1),
     'L0_ffn_heavy_b2': (0.0, 0.1)}
    factors = {}
    for name, (base, spread) in spreads.items():
        noise = np.random.default_rng([zlib.crc32(name.encode()), seed]).standard_normal(out[name].shape)
        drawn = base * np.exp(spread * noise) if base else spread * noise
        out[name] = jnp.asarray(drawn.astype(out[name].dtype))
    for name, factor in factors.items():
        out[name] = (out[name] * factor).astype(out[name].dtype)
    return out
```

```python
from contextlib import ExitStack

import numpy as np

import concourse.bass as bass
from concourse import mybir

ALU = mybir.AluOpType
ACT = mybir.ActivationFunctionType
F32 = mybir.dt.float32
F32R = mybir.dt.float32r
U8 = mybir.dt.uint8
AX_X = mybir.AxisListType.X

P = 128
B = 16
N = 256
D = 256
DC = 192
HEADS = 4
DH = 64
KEYS = 2 * N
TT = N // P
KT = KEYS // P
TILES = B * TT
PAIRS = B // 2
HID_L = 128
HID_H = 1024
HT = (HID_L + HID_H) // P
ITERS = 50
LN_EPS = 1e-5
BIG = 3.0e38


def build(nc, x, ctx_in, mask, w_lat, w_ctx, w_o, w1, w2, vec_k, vec_c, vec_h, rows, eye, out):
    ctx = ExitStack()
    with ctx:
        def sb(name, shape, dt=F32):
            return ctx.enter_context(nc.sbuf_tensor(name, shape, dt))

        def sem(name):
            return ctx.enter_context(nc.semaphore(name))

        bank = [ctx.enter_context(nc.psum_tensor(f"bank{i}", [P, 512], F32)) for i in range(8)]

        x_all = sb("x_all", [P, TILES, D])
        ident = sb("ident", [P, P])
        wlat_hi = sb("wlat_hi", [P, 2, 3 * D], F32R)
        wlat_lo = sb("wlat_lo", [P, 2, 3 * D], F32R)
        wctx_hi = sb("wctx_hi", [P, 2, 2 * D], F32R)
        wctx_lo = sb("wctx_lo", [P, 2, 2 * D], F32R)
        wo = sb("wo", [P, 2, D])
        w1_hi = sb("w1_hi", [P, 2, HT * P], F32R)
        w1_lo = sb("w1_lo", [P, 2, HT * P], F32R)
        w2_hi = sb("w2_hi", [P, HT, D], F32R)
        w2_lo = sb("w2_lo", [P, HT, D], F32R)
        vk = sb("vk", [P, 6])
        vc = sb("vc", [P, 4])
        vh = sb("vh", [P, 4 + HT])
        row_b = sb("row_b", [P, 4, D])
        neg_half = sb("neg_half", [P, 32])
        neg_gqk = sb("neg_gqk", [P, 1])
        rt_sum = sb("rt_sum", [P, 1])
        stats2 = sb("stats2", [P, TILES, 2])
        dots = sb("dots", [P, TILES])
        mask_all = sb("mask_all", [P, B * N], U8)

        c_in = [sb(f"c_in{p}", [P, TT, DC]) for p in range(2)]
        st6 = sb("st6", [P, 4, 6])
        mv = sb("mv", [P, 4, 2])
        rstd = sb("rstd", [P, 4])
        ln = sb("ln", [P, TT, D])
        cn = sb("cn", [P, TT, DC + 64])
        lnT = sb("lnT", [P, 2, N])
        lnT_hi = sb("lnT_hi", [P, 2, N], F32R)
        lnT_lo = sb("lnT_lo", [P, 2, N], F32R)
        cT = sb("cT", [P, 2, N])
        cT_hi = sb("cT_hi", [P, 2, N], F32R)
        cT_lo = sb("cT_lo", [P, N], F32R)
        qk = sb("qk", [P, TT, 2 * D])
        kc = sb("kc", [P, TT, D])
        sq = sb("sq", [P, 6, D])
        ss = sb("ss", [P, 6 * HEADS])
        rr = sb("rr", [P, 6 * HEADS])
        v_aug = [sb(f"v_aug{p}", [P, KT, HEADS, DH + 1]) for p in range(2)]
        qT = sb("qT", [P, 2, N])
        kT = sb("kT", [P, 2, KEYS])
        maskb = [sb(f"maskb{p}", [P, KEYS]) for p in range(2)]
        prob = sb("prob", [P, TT * HEADS, KEYS])
        mn = sb("mn", [P, TT * HEADS])
        probT = sb("probT", [P, 4, KT, P])
        rden = sb("rden", [P, HEADS])
        o_n = sb("o_n", [P, TT, D])
        o_T = sb("o_T", [P, 2, N])

        z = prob[:, 0:2, :].rearrange("p a b -> p (a b)").rearrange("p (j d) -> p j d", j=4)
        zT_hi = sb("zT_hi", [P, 2, 512], F32R)
        zT_lo = sb("zT_lo", [P, 2, 512], F32R)
        h_raw = [prob[:, 2 + i, :] for i in range(3)]
        h_hi = [sb(f"h_hi{i}", [P, 512], F32R) for i in range(3)]
        h_lo = [sb(f"h_lo{i}", [P, 512], F32R) for i in range(3)]
        hv = probT[:, :, :, :].rearrange("p a b c -> p (a b c)")[:, 0:4 * D].rearrange("p (a d) -> p a d", a=4)
        r2 = sb("r2", [P, TILES])
        zs = sb("zs", [P, TILES])
        sm = sb("sm", [P, TILES])
        s_tok = sb("s_tok", [P, TILES])
        cred = sb("cred", [P, 2])
        s16 = sb("s16", [B, N])
        e16 = sb("e16", [B, N])
        m16 = sb("m16", [B, N])
        cc = sb("cc", [B, 4])
        sel = sb("sel", [P, TT, B])

        w1_raw = prob[:, 0:5, :].rearrange("p a b -> p (a b)")[:, 0:2 * HT * P].rearrange("p (k n) -> p k n", k=2)
        wctx_raw = prob[:, 5:7, :].rearrange("p a b -> p (a b)").rearrange("p (k n) -> p k n", k=2)
        wlat_raw = sq[:, :, :].rearrange("p a b -> p (a b)").rearrange("p (k n) -> p k n", k=2)
        w2_raw_a = probT[:, :, :, :].rearrange("p a b c -> p (a b c)").rearrange("p (a d) -> p a d", a=8)
        w2_raw_b = prob[:, 7, 0:D]

        consts_in = sem("consts_in")
        wlat_in, wctx_in, w1_in, w2_in, wo_in, mask_in = (sem(s) for s in (
            "wlat_in", "wctx_in", "w1_in", "w2_in", "wo_in", "mask_in"))
        batch_in = [sem(f"batch_in{p}") for p in range(2)]
        out_done = sem("out_done")
        setup_v, setup_p = sem("setup_v"), sem("setup_p")
        kinds = ("lnT", "cT", "qk0", "qk1", "v01", "kv0", "kv1", "qT", "kT0", "kT1", "oT", "y")
        ps = {k: sem(k + "_ps") for k in kinds}
        rd = {k: sem(k + "_sb") for k in kinds}
        mv_ready, rstd_ready, ln_ready, small_v = sem("mv_ready"), sem("rstd_ready"), sem("ln_ready"), sem("small_v")
        pool_step, pool_step2 = sem("pool_step"), sem("pool_step2")
        lnT_hi_ready, lnT_lo_ready = sem("lnT_hi_ready"), sem("lnT_lo_ready")
        cT_hi_ready, cT_stacked, cT_lo_ready = sem("cT_hi_ready"), sem("cT_stacked"), sem("cT_lo_ready")
        ss_lat, ss_ctx, rr_lat, rr_ctx = sem("ss_lat"), sem("ss_ctx"), sem("rr_lat"), sem("rr_ctx")
        lat_scaled, ctx_scaled = sem("lat_scaled"), sem("ctx_scaled")
        mask_ready, xbo_ready = sem("mask_ready"), sem("xbo_ready")
        s_ps, s_masked, p_ready = sem("s_ps"), sem("s_masked"), sem("p_ready")
        pt_ps = sem("pt_ps")
        pt_even, pt_odd = sem("pt_even"), sem("pt_odd")
        pv_done, o_rcp, o_sb = sem("pv_done"), sem("o_rcp"), sem("o_sb")
        x2_stats = sem("x2_stats")
        zs_ready, s_ready, s16_ps, e_ready, exp_ready, sel16_ready, sel_ps, sel_ready = (sem(s) for s in (
            "zs_ready", "s_ready", "s16_ps", "e_ready", "exp_ready", "sel16_ready", "sel_ps", "sel_ready"))
        descent_v, c_sum, c_ready = sem("descent_v"), sem("c_sum"), sem("c_ready")
        turn_v, turn_p = sem("turn_v"), sem("turn_p")
        x_biased, norm_step, tail_step = sem("x_biased"), sem("norm_step"), sem("tail_step")
        z_ready, zT_ps, zT_hi_s, zT_lo_s = sem("z_ready"), sem("zT_ps"), sem("zT_hi_s"), sem("zT_lo_s")
        h_ps, gelu_done, h_hi_s, h_lo_s, h_used, acc_sb, fin = (sem(s) for s in (
            "h_ps", "gelu_done", "h_hi_s", "h_lo_s", "h_used", "acc_sb", "fin"))

        kind_bank = {k: bank[i] for k, i in zip(kinds, (1, 2, 0, 1, 2, 0, 1, 2, 0, 2, 1, 0))}
        kind_bank["oT"], kind_bank["kT1"] = bank[1], bank[2]
        s_bank = [bank[3], bank[4]]
        pt_bank = [bank[5], bank[6]]
        o_bank = bank[7]

        x_t = x.rearrange("b (j p) d -> p (b j) d", p=P)
        out_t = out.rearrange("b (j p) d -> p (b j) d", p=P)
        c_t = ctx_in.rearrange("b (j p) d -> p (b j) d", p=P)

        block = ctx.enter_context(nc.Block())

        @block.sync
        def _(sp):
            def load(b, p):
                sp.dma_start(x_all[:, bass.ds(2 * b, TT), :], x_t[:, bass.ds(2 * b, TT), :]).then_inc(batch_in[p], 16)
                sp.dma_start(c_in[p][:, :, :], c_t[:, bass.ds(2 * b, TT), :]).then_inc(batch_in[p], 16)

            load(0, 0)
            load(1, 1)
            sp.dma_start(wlat_raw, w_lat.rearrange("(k p) n -> p k n", p=P)).then_inc(wlat_in, 16)
            sp.dma_start(wctx_raw, w_ctx.rearrange("(k p) n -> p k n", p=P)).then_inc(wctx_in, 16)
            sp.dma_start(mask_all[:, :], mask.rearrange("(o b) n -> o (b n)", o=1).broadcast_to([P, B * N])).then_inc(mask_in, 16)
            sp.dma_start(wo[:, :, :], w_o.rearrange("(k p) n -> p k n", p=P)).then_inc(wo_in, 16)
            sp.dma_start(w1_raw, w1.rearrange("(k p) n -> p k n", p=P)).then_inc(w1_in, 16)
            w2_t = w2.rearrange("(k p) n -> p k n", p=P)
            sp.dma_start(w2_raw_a, w2_t[:, 0:8, :]).then_inc(w2_in, 16)
            sp.dma_start(w2_raw_b, w2_t[:, 8, :]).then_inc(w2_in, 16)
            with sp.Fori(1, B // 2) as i:
                for p in range(2):
                    sp.wait_ge(ln_ready, 2 * i + p - 1)
                    load(2 * i + p, p)
            with sp.Fori(0, PAIRS) as g:
                sp.wait_ge(fin, g + 1)
                sp.dma_start(out_t[:, bass.ds(4 * g, 4), :], x_all[:, bass.ds(4 * g, 4), :]).then_inc(out_done, 16)
            sp.wait_ge(out_done, 16 * PAIRS)

        @block.tensor
        def _(pe):
            def take(kind, need):
                if need is not None:
                    pe.wait_ge(rd[need[0]], need[1])

            def split_products(dst, pairs):
                for n, (shi, slo, mhi, mlo) in enumerate(pairs):
                    terms = [(shi, mhi), (shi, mlo)] + ([(slo, mhi)] if slo is not None else [])
                    for m, (s, v) in enumerate(terms):
                        last = pe.matmul(dst, s, v, start=(n == 0 and m == 0),
                                         stop=(n == len(pairs) - 1 and m == len(terms) - 1))
                return last

            def front_transposes(f, need_ln, need_c):
                pe.wait_ge(ln_ready, f + 1)
                take("lnT", need_ln)
                for kt in range(2):
                    for j in range(TT):
                        last = pe.transpose(kind_bank["lnT"][:, kt * N + j * P:kt * N + (j + 1) * P],
                                            ln[:, j, kt * P:(kt + 1) * P], ident[:, :])
                last.then_inc(ps["lnT"], 1)
                take("cT", need_c)
                for kt in range(2):
                    for j in range(TT):
                        last = pe.transpose(kind_bank["cT"][:, kt * N + j * P:kt * N + (j + 1) * P],
                                            cn[:, j, kt * P:(kt + 1) * P], ident[:, :])
                last.then_inc(ps["cT"], 1)

            def lat_pairs(j, c0, c1):
                t = slice(j * P, (j + 1) * P)
                return [(lnT_hi[:, kt, t], lnT_lo[:, kt, t], wlat_hi[:, kt, c0:c1], wlat_lo[:, kt, c0:c1])
                        for kt in range(2)]

            def project(f, need_qk0):
                pe.wait_ge(lnT_hi_ready, f + 1)
                pe.wait_ge(lnT_lo_ready, f + 1)
                take("qk0", need_qk0)
                split_products(kind_bank["qk0"][:, :], lat_pairs(0, 0, 2 * D)).then_inc(ps["qk0"], 1)
                take("qk1", ("lnT", f + 1))
                split_products(kind_bank["qk1"][:, :], lat_pairs(1, 0, 2 * D)).then_inc(ps["qk1"], 1)
                take("v01", ("cT", f + 1))
                for j in range(TT):
                    last = split_products(kind_bank["v01"][:, j * D:(j + 1) * D], lat_pairs(j, 2 * D, 3 * D))
                last.then_inc(ps["v01"], 1)
                pe.wait_ge(cT_stacked, f + 1)
                pe.wait_ge(cT_lo_ready, f + 1)
                for j in range(TT):
                    take(f"kv{j}", (f"qk{j}", f + 1))
                    t = slice(j * P, (j + 1) * P)
                    dst = kind_bank[f"kv{j}"][:, :]
                    pe.matmul(dst, cT_hi[:, 1, t], wctx_hi[:, 1, :], start=True, stop=False)
                    pe.matmul(dst, cT_hi[0:DH, 1, t], wctx_lo[0:DH, 1, :], start=False, stop=False)
                    pe.matmul(dst, cT_hi[:, 0, t], wctx_hi[:, 0, :], start=False, stop=False)
                    pe.matmul(dst, cT_hi[:, 0, t], wctx_lo[:, 0, :], start=False, stop=False)
                    pe.matmul(dst, cT_lo[:, t], wctx_hi[:, 0, :], start=False, stop=True).then_inc(ps[f"kv{j}"], 1)

            def q_transposes(f):
                pe.wait_ge(lat_scaled, f + 1)
                take("qT", ("v01", f + 1))
                for c in range(2):
                    for j in range(TT):
                        last = pe.transpose(kind_bank["qT"][:, c * N + j * P:c * N + (j + 1) * P],
                                            qk[:, j, c * P:(c + 1) * P], ident[:, :])
                last.then_inc(ps["qT"], 1)

            def k_transposes(f, c, need):
                if c == 0:
                    pe.wait_ge(ctx_scaled, f + 1)
                take(f"kT{c}", need)
                for t in range(KT):
                    src = qk[:, t, D + c * P:D + (c + 1) * P] if t < TT else kc[:, t - TT, c * P:(c + 1) * P]
                    last = pe.transpose(kind_bank[f"kT{c}"][:, t * P:(t + 1) * P], src, ident[:, :])
                last.then_inc(ps[f"kT{c}"], 1)

            def scores(t, qt):
                if qt == 0:
                    for k in ("qT", "kT0", "kT1"):
                        pe.wait_ge(rd[k], t + 1)
                for h in range(HEADS):
                    u = qt * HEADS + h
                    pe.wait_ge(s_masked, 8 * t + u + 1)
                    r = slice(DH * (h % 2), DH * (h % 2) + DH)
                    pe.matmul(s_bank[h % 2][:, :], qT[r, h // 2, qt * P:(qt + 1) * P], kT[r, h // 2, :],
                              start=True, stop=True).then_inc(s_ps, 1)

            def prob_transposes(t, u):
                pe.wait_ge(p_ready, 8 * t + u + 1)
                pe.wait_ge(pt_even if u % 2 == 0 else pt_odd, 4 * t + u // 2 + 1)
                for k in range(KT):
                    last = pe.transpose(pt_bank[u % 2][:, k * P:(k + 1) * P], prob[:, u, k * P:(k + 1) * P], ident[:, :])
                last.then_inc(pt_ps, 1)

            def weighted_values(t, u, p):
                qt, h = divmod(u, HEADS)
                pe.wait_ge(pt_even if u % 2 == 0 else pt_odd, 4 * t + u // 2 + 2)
                if u == 0:
                    pe.wait_ge(rd["v01"], t + 1)
                    pe.wait_ge(rd["kv1"], t + 1)
                if h == 0:
                    pe.wait_ge(o_sb, 2 * t + qt + 1)
                for k in range(KT):
                    last = pe.matmul(o_bank[:, h * (DH + 1):(h + 1) * (DH + 1)], probT[:, u % 4, k, :],
                                     v_aug[p][:, k, h, :], start=(k == 0), stop=(k == KT - 1))
                last.then_inc(pv_done, 1)

            def attend(t, p):
                prob_transposes(t, 0)
                for u in range(1, 8):
                    prob_transposes(t, u)
                    weighted_values(t, u - 1, p)
                weighted_values(t, 7, p)

            def o_transposes(t, need):
                pe.wait_ge(o_sb, 2 * t + 3)
                take("oT", need)
                for c in range(2):
                    for j in range(TT):
                        last = pe.transpose(kind_bank["oT"][:, c * N + j * P:c * N + (j + 1) * P],
                                            o_n[:, j, c * P:(c + 1) * P], ident[:, :])
                last.then_inc(ps["oT"], 1)

            def out_projection(t, need):
                pe.wait_ge(rd["oT"], t + 2)
                take("y", need)
                for j in range(TT):
                    for c in range(2):
                        last = pe.matmul(kind_bank["y"][:, j * D:(j + 1) * D], o_T[:, c, j * P:(j + 1) * P],
                                         wo[:, c, :], start=(c == 0), stop=(c == 1))
                last.then_inc(ps["y"], 1)

            pe.wait_ge(consts_in, 16 * 5)
            front_transposes(0, None, None)
            pe.wait_ge(setup_v, 6)
            project(0, None)
            q_transposes(0)
            k_transposes(0, 0, ("kv0", 1))
            k_transposes(0, 1, ("qT", 1))
            pe.wait_ge(wo_in, 16)

            def step(t, p):
                f = t + 1
                scores(t, 0)
                front_transposes(f, ("oT", t + 1), ("kT1", t + 1))
                scores(t, 1)
                project(f, ("y", t + 1))
                attend(t, p)
                q_transposes(f)
                k_transposes(f, 0, ("kv0", f + 1))
                o_transposes(t, ("kv1", f + 1))
                k_transposes(f, 1, ("qT", f + 1))
                out_projection(t, ("kT0", f + 1))

            with pe.Fori(0, (B - 2) // 2) as i:
                step(2 * i, 0)
                step(2 * i + 1, 1)
            step(B - 2, 0)
            scores(B - 1, 0)
            scores(B - 1, 1)
            attend(B - 1, 1)
            o_transposes(B - 1, None)
            out_projection(B - 1, ("y", B))

            acc = bank[0:4]
            h_bank = bank[4:7]
            zT_bank = bank[7]

            def z_transposes(g, kt):
                pe.wait_ge(z_ready, g + 1)
                pe.wait_ge(zT_lo_s, 2 * g + kt + 1)
                for j in range(4):
                    last = pe.transpose(zT_bank[:, j * P:(j + 1) * P], z[:, j, kt * P:(kt + 1) * P], ident[:, :])
                last.then_inc(zT_ps, 1)

            def hidden(g, m):
                if m == 0:
                    pe.wait_ge(zT_lo_s, 2 * g + 3)
                    pe.wait_ge(zT_hi_s, 2 * g + 2)
                pe.wait_ge(gelu_done, HT * g + m + 1)
                t = slice(m * P, (m + 1) * P)
                split_products(h_bank[m % 3][:, :],
                               [(w1_hi[:, k, t], w1_lo[:, k, t], zT_hi[:, k, :], zT_lo[:, k, :]) for k in range(2)]
                               ).then_inc(h_ps, 1)

            def outputs(g, m):
                pe.wait_ge(h_hi_s, HT * g + m + 1)
                pe.wait_ge(h_lo_s, HT * g + m + 1)
                if m == 0:
                    pe.wait_ge(acc_sb, g + 1)
                c = slice(0, D) if m == 0 else slice(D, 2 * D)
                for j in range(4):
                    t = slice(j * P, (j + 1) * P)
                    terms = ((h_hi[m % 3][:, t], w2_hi[:, m, :]), (h_hi[m % 3][:, t], w2_lo[:, m, :]),
                             (h_lo[m % 3][:, t], w2_hi[:, m, :]))
                    for n, (s, v) in enumerate(terms):
                        last = pe.matmul(acc[j][:, c], s, v, start=(m <= 1 and n == 0),
                                         stop=(m in (0, HT - 1) and n == 2))
                last.then_inc(h_used, 1)

            def ffn(g, more=True):
                hidden(g, 0)
                hidden(g, 1)
                for m in range(HT):
                    if m + 2 < HT:
                        hidden(g, m + 2)
                    if more and m >= HT - 2:
                        z_transposes(g + 1, m - (HT - 2))
                    outputs(g, m)

            pe.wait_ge(x2_stats, 1)
            pe.wait_ge(s_ready, 1)
            for j in range(TT):
                last = pe.transpose(bank[3][0:B, j * P:(j + 1) * P], s_tok[:, j:TILES:TT], ident[:, :])
            last.then_inc(s16_ps, 1)
            for kt in range(2):
                z_transposes(0, kt)
            pe.wait_ge(exp_ready, 1)
            ffn(0)
            pe.wait_ge(sel16_ready, 1)
            pe.wait_ge(gelu_done, HT + 3)
            for j in range(TT):
                last = pe.transpose(bank[4][:, j * B:(j + 1) * B], s16[:, j * P:(j + 1) * P], ident[0:B, 0:B])
            last.then_inc(sel_ps, 1)
            pe.wait_ge(sel_ready, 1)
            with pe.Fori(1, PAIRS - 1) as g:
                ffn(g)
            ffn(PAIRS - 1, more=False)

        @block.vector
        def _(dve):
            dve.wait_ge(wlat_in, 16)
            dve.tensor_copy(wlat_hi[:, :, :], wlat_raw).then_inc(setup_v, 1)
            dve.wait_ge(wctx_in, 16)
            dve.tensor_copy(wctx_hi[:, :, :], wctx_raw).then_inc(setup_v, 1)
            dve.wait_ge(setup_v, 2)
            dve.tensor_sub(wlat_lo[:, :, :], wlat_raw, wlat_hi[:, :, :].bitcast(F32)).then_inc(setup_v, 1)
            dve.tensor_sub(wctx_lo[:, :, :], wctx_raw, wctx_hi[:, :, :].bitcast(F32)).then_inc(setup_v, 1)
            dve.wait_ge(consts_in, 16 * 5)
            dve.tensor_tensor(neg_gqk[:, :], vk[:, 4:5], vk[:, 5:6], ALU.mult).then_inc(setup_v, 1)
            dve.wait_ge(setup_v, 5)
            dve.tensor_scalar(neg_gqk[:, :], neg_gqk[:, :], -float(DH) ** -0.5, None, ALU.mult).then_inc(setup_v, 1)
            dve.wait_ge(setup_v, 6)
            dve.memset(v_aug[0][:, :, :, DH:DH + 1], 1.0).then_inc(s_masked, 1)
            dve.memset(v_aug[1][:, :, :, DH:DH + 1], 1.0).then_inc(s_masked, 1)
            dve.memset(mn[:, :], 0.0).then_inc(pt_even, 1)
            dve.memset(rden[:, :], 0.0).then_inc(o_sb, 1)
            dve.memset(cc[:, :], 1.0).then_inc(rd["oT"], 1)
            dve.memset(m16[:, :], 0.0).then_inc(c_ready, 1)
            dve.memset(sm[:, :], 0.0).then_inc(rd["y"], 1)
            dve.memset(zs[:, :], 0.0).then_inc(acc_sb, 1)
            dve.memset(r2[:, :], 0.0).then_inc(zT_lo_s, 1)

            def moments(b, p, bp):
                dve.wait_ge(batch_in[p], 32 * (bp + 1))
                for j in range(TT):
                    dve.bn_stats(st6[:, j, :], x_all[:, bass.ds(2 * b + j, 1), :].rearrange("p a d -> p (a d)"))
                    dve.bn_stats(st6[:, TT + j, :], c_in[p][:, j, :]).then_inc(small_v, 1)
                dve.wait_ge(small_v, 2 * b + 2)
                dve.sem_inc(turn_v)
                for j in range(4):
                    last = dve.bn_aggr(mv[:, j, :], st6[:, j, :])
                last.then_inc(mv_ready, 1)

            def normalise(b, p, first=False):
                dve.wait_ge(rstd_ready, b + 1)
                if not first:
                    dve.wait_ge(ps["cT"], b)
                for j in range(TT):
                    dve.tensor_scalar(ln[:, j, :], x_all[:, bass.ds(2 * b + j, 1), :].rearrange("p a d -> p (a d)"),
                                      mv[:, j, 0:1], rstd[:, j:j + 1], ALU.subtract, ALU.mult)
                    dve.tensor_scalar(cn[:, j, 0:DC], c_in[p][:, j, :],
                                      mv[:, TT + j, 0:1], rstd[:, TT + j:TT + j + 1], ALU.subtract, ALU.mult)
                    last = dve.tensor_scalar(cn[:, j, DC:DC + 64], c_in[p][:, j, P:DC],
                                             mv[:, TT + j, 0:1], rstd[:, TT + j:TT + j + 1], ALU.subtract, ALU.mult)
                last.then_inc(ln_ready, 1)

            def high_parts(f):
                dve.wait_ge(rd["lnT"], f + 1)
                dve.tensor_copy(lnT_hi[:, :, :], lnT[:, :, :]).then_inc(lnT_hi_ready, 1)
                dve.wait_ge(rd["cT"], f + 1)
                dve.tensor_copy(cT_hi[:, :, :], cT[:, :, :]).then_inc(cT_hi_ready, 1)
                dve.wait_ge(cT_hi_ready, f + 1)
                dve.tensor_tensor(cT_hi[DH:P, 1, :], cT[DH:P, 1, :], cT_hi[DH:P, 1, :].bitcast(F32), ALU.subtract
                                  ).then_inc(cT_stacked, 1)

            def latent_values(f, fp):
                dve.wait_ge(ps["v01"], f + 1)
                dve.tensor_copy(v_aug[fp][:, 0:TT, :, 0:DH],
                                kind_bank["v01"][:, :].rearrange("p (j h d) -> p j h d", j=TT, h=HEADS)
                                ).then_inc(rd["v01"], 1)

            def square_sums_lat(f):
                dve.wait_ge(rd["qk1"], f + 1)
                dve.tensor_reduce(ss[:, 0:16], sq[:, 0:4, :].rearrange("p a (h d) -> p (a h) d", d=DH),
                                  AX_X, ALU.add).then_inc(ss_lat, 1)

            def scale_lat(f):
                dve.wait_ge(rr_lat, f + 1)
                v = qk[:, :, :].rearrange("p j (h d) -> p (j h) d", d=DH)
                dve.tensor_tensor(v, v, rr[:, 0:16].rearrange("p (h o) -> p h o", o=1).broadcast_to([P, 16, DH]),
                                  ALU.mult).then_inc(lat_scaled, 1)

            def square_sums_ctx(f):
                dve.wait_ge(rd["kv1"], f + 1)
                dve.tensor_reduce(ss[:, 16:24], sq[:, 4:6, :].rearrange("p a (h d) -> p (a h) d", d=DH),
                                  AX_X, ALU.add).then_inc(ss_ctx, 1)

            def mask_and_min(t, qt, p):
                if qt == 0:
                    dve.wait_ge(mask_ready, t + 1)
                for h in range(HEADS):
                    u = qt * HEADS + h
                    dve.wait_ge(s_ps, 8 * t + u + 1)
                    dve.sem_inc(turn_v)
                    dve.tensor_tensor_reduce(prob[:, u, :], s_bank[h % 2][:, :], maskb[p][:, :], 1.0, BIG,
                                             ALU.add, ALU.min, mn[:, u:u + 1]).then_inc(s_masked, 1)

            def probT_even(t, u):
                dve.wait_ge(pt_ps, 8 * t + u + 1)
                if u >= 4:
                    dve.wait_ge(pv_done, 8 * t + u - 3)
                dve.tensor_copy(probT[:, u % 4, :, :].rearrange("p k q -> p (k q)"), pt_bank[0][:, :]
                                ).then_inc(pt_even, 1)

            def normalise_out(t, qt):
                dve.wait_ge(pv_done, 8 * t + 4 * qt + 4)
                o = o_bank[:, 0:HEADS * (DH + 1)].rearrange("p (h d) -> p h d", d=DH + 1)
                dve.reciprocal(rden[:, :], o[:, :, DH:DH + 1].rearrange("p h o -> p (h o)")).then_inc(o_rcp, 1)
                dve.wait_ge(o_rcp, 2 * t + qt + 1)
                dve.tensor_tensor(o_n[:, qt, :].rearrange("p (h d) -> p h d", d=DH), o[:, :, 0:DH],
                                  rden[:, :].rearrange("p (h o) -> p h o", o=1).broadcast_to([P, HEADS, DH]),
                                  ALU.mult).then_inc(o_sb, 1)

            def qT_out(f):
                dve.wait_ge(ps["qT"], f + 1)
                dve.tensor_scalar(qT[:, :, :].rearrange("p c n -> p (c n)"), kind_bank["qT"][:, :],
                                  neg_gqk[:, 0:1], None, ALU.mult).then_inc(rd["qT"], 1)

            def kT_out(f, c):
                dve.wait_ge(ps[f"kT{c}"], f + 1)
                dve.tensor_copy(kT[:, c, :], kind_bank[f"kT{c}"][:, :]).then_inc(rd[f"kT{c}"], 1)

            def oT_out(t):
                dve.wait_ge(ps["oT"], t + 1)
                dve.tensor_copy(o_T[:, :, :].rearrange("p c n -> p (c n)"), kind_bank["oT"][:, :]).then_inc(rd["oT"], 1)

            def residual(t):
                dve.wait_ge(ps["y"], t + 1)
                dve.wait_ge(xbo_ready, t + 1)
                xt = x_all[:, bass.ds(2 * t, TT), :].rearrange("p j d -> p (j d)")
                dve.tensor_tensor(xt, kind_bank["y"][:, :], xt, ALU.add).then_inc(rd["y"], 1)

            def step_f(t, p, last=False):
                f = t + 1
                mask_and_min(t, 0, p)
                high_parts(f)
                mask_and_min(t, 1, p)
                latent_values(f, 1 - p)
                square_sums_lat(f)
                probT_even(t, 0)
                scale_lat(f)
                probT_even(t, 2)
                square_sums_ctx(f)
                probT_even(t, 4)
                normalise_out(t, 0)
                probT_even(t, 6)
                return f

            def step(t, p, th, next_ln=True):
                f = step_f(t, p)
                if next_ln:
                    moments(t + 2, p, th)
                normalise_out(t, 1)
                qT_out(f)
                kT_out(f, 0)
                oT_out(t)
                kT_out(f, 1)
                if next_ln:
                    normalise(t + 2, p)
                residual(t)

            moments(0, 0, 0)
            normalise(0, 0, first=True)
            high_parts(0)
            latent_values(0, 0)
            square_sums_lat(0)
            scale_lat(0)
            square_sums_ctx(0)
            moments(1, 1, 0)
            normalise(1, 1)
            qT_out(0)
            kT_out(0, 0)
            kT_out(0, 1)
            dve.wait_ge(w1_in, 16)
            for k in range(2):
                dve.tensor_scalar(w1_raw[:, k, 0:HID_L], w1_raw[:, k, 0:HID_L], vh[:, k:k + 1], None, ALU.mult)
                dve.tensor_scalar(w1_raw[:, k, HID_L:], w1_raw[:, k, HID_L:], vh[:, 2 + k:3 + k], None,
                                  ALU.mult).then_inc(setup_v, 1)
            dve.wait_ge(setup_v, 8)
            dve.tensor_copy(w1_hi[:, :, :], w1_raw).then_inc(setup_v, 1)
            dve.wait_ge(w2_in, 32)
            dve.tensor_copy(w2_hi[:, 0:8, :], w2_raw_a).then_inc(setup_v, 1)
            dve.tensor_copy(w2_hi[:, 8, :], w2_raw_b).then_inc(setup_v, 1)
            dve.wait_ge(setup_v, 11)
            dve.tensor_sub(w1_lo[:, :, :], w1_raw, w1_hi[:, :, :].bitcast(F32)).then_inc(setup_v, 1)
            dve.tensor_sub(w2_lo[:, 0:8, :], w2_raw_a, w2_hi[:, 0:8, :].bitcast(F32)).then_inc(setup_v, 1)
            dve.tensor_sub(w2_lo[:, 8, :], w2_raw_b, w2_hi[:, 8, :].bitcast(F32)).then_inc(setup_v, 1)
            dve.wait_ge(setup_v, 14)
            dve.tensor_reduce(rt_sum[:, :], row_b[:, 3, :], AX_X, ALU.add).then_inc(setup_v, 1)

            with dve.Fori(0, (B - 2) // 2) as i:
                step(2 * i, 0, i + 1)
                step(2 * i + 1, 1, i + 1)
            step(B - 2, 0, None, next_ln=False)
            mask_and_min(B - 1, 0, 1)
            mask_and_min(B - 1, 1, 1)
            for u in (0, 2, 4):
                probT_even(B - 1, u)
            normalise_out(B - 1, 0)
            probT_even(B - 1, 6)
            normalise_out(B - 1, 1)
            oT_out(B - 1)
            residual(B - 1)

            dve.wait_ge(rd["y"], B + 1)
            for t in range(TILES):
                dve.bn_stats(sq[:, 0, 6 * t:6 * t + 6], x_all[:, t, :])
                last = dve.tensor_tensor_reduce(prob[:, 0, 0:D], x_all[:, t, :], row_b[:, 3, :], 1.0, 0.0,
                                                ALU.mult, ALU.add, dots[:, t:t + 1])
                last.then_inc(descent_v, 1)
                dve.wait_ge(descent_v, t + 1)
            for t in range(TILES):
                last = dve.bn_aggr(stats2[:, t, :], sq[:, 0, 6 * t:6 * t + 6])
            last.then_inc(x2_stats, 1)
            dve.wait_ge(zs_ready, 1)
            dve.wait_ge(x2_stats, 1)
            dve.tensor_scalar(sm[:, :], stats2[:, :, 0:1].rearrange("p t o -> p (t o)"), rt_sum[:, 0:1], None,
                              ALU.mult).then_inc(descent_v, 1)
            dve.wait_ge(descent_v, TILES + 1)
            dve.tensor_tensor(sm[:, :], dots[:, :], sm[:, :], ALU.subtract).then_inc(descent_v, 1)
            dve.wait_ge(descent_v, TILES + 2)
            dve.tensor_tensor(s_tok[:, :], sm[:, :], r2[:, :], ALU.mult).then_inc(s_ready, 1)

            def z_tiles(g):
                for j in range(4):
                    last = dve.tensor_scalar(z[:, j, :], x_all[:, bass.ds(4 * g + j, 1), :].rearrange("p a d -> p (a d)"),
                                             stats_col(g, j, 0), zs_col(g, j), ALU.subtract, ALU.mult)
                last.then_inc(z_ready, 1)

            def stats_col(g, j, k):
                return stats2[:, bass.ds(4 * g + j, 1), k:k + 1].rearrange("p a o -> p (a o)")

            def zs_col(g, j):
                return zs[:, bass.ds(4 * g + j, 1)]

            def zT_low(g):
                for kt in range(2):
                    dve.wait_ge(zT_hi_s, 2 * g + kt + 1)
                    dve.tensor_tensor(zT_lo[:, kt, :], bank[7][:, :], zT_hi[:, kt, :].bitcast(F32), ALU.subtract
                                      ).then_inc(zT_lo_s, 1)

            def h_low(g, m):
                dve.wait_ge(h_hi_s, HT * g + m + 1)
                dve.tensor_tensor(h_lo[m % 3][:, :], h_raw[m % 3], h_hi[m % 3][:, :].bitcast(F32), ALU.subtract
                                  ).then_inc(h_lo_s, 1)

            def sums_out(g):
                dve.wait_ge(h_used, HT * (g + 1))
                for j in range(4):
                    xt = x_all[:, bass.ds(4 * g + j, 1), :].rearrange("p a d -> p (a d)")
                    dve.tensor_tensor(xt, bank[j][:, 0:D], xt, ALU.add)
                    last = dve.tensor_tensor(hv[:, j, :], bank[j][:, D:2 * D], row_b[:, 2, :], ALU.add)
                last.then_inc(acc_sb, 1)

            def final(g):
                dve.wait_ge(acc_sb, g + 2)
                for j in range(4):
                    xt = x_all[:, bass.ds(4 * g + j, 1), :].rearrange("p a d -> p (a d)")
                    last = dve.scalar_tensor_tensor(xt, hv[:, j, :], sel[:, j % TT, bass.ds(2 * g + j // TT, 1)], xt,
                                                    ALU.mult, ALU.add)
                last.then_inc(fin, 1)

            def ffn(g, first=False, more=True):
                for m in range(HT):
                    h_low(g, m)
                    if m == 2 and more:
                        z_tiles(g + 1)
                    if m == 4 and not first:
                        final(g - 1)
                    if first:
                        descent((ITERS - 1) * m // HT, (ITERS - 1) * (m + 1) // HT)
                if first:
                    multiplier()
                if more:
                    zT_low(g + 1)
                sums_out_pre(g)
                sums_out(g)

            def descent(lo, hi):
                with dve.Fori(lo, hi) as it:
                    dve.wait_ge(c_ready, it + 1)
                    dve.tensor_scalar(m16[:, :], e16[:, :], cc[:, 0:1], None, ALU.min, ALU.add, accum_out=cc[:, 2:3]
                                      ).then_inc(c_sum, 1)
                    dve.wait_ge(c_sum, it + 1)
                    dve.tensor_scalar(cc[:, 0:1], cc[:, 2:3], 1.0 / N, 1e-37, ALU.mult, ALU.max).then_inc(c_ready, 1)

            def multiplier():
                dve.wait_ge(c_ready, ITERS)
                dve.reciprocal(cc[:, 3:4], cc[:, 0:1]).then_inc(c_ready, 1)
                dve.wait_ge(c_ready, ITERS + 1)
                dve.tensor_scalar(m16[:, :], e16[:, :], cc[:, 3:4], 1.0, ALU.mult, ALU.min).then_inc(c_ready, 1)
                dve.wait_ge(c_ready, ITERS + 2)
                dve.tensor_scalar(s16[:, :], m16[:, :], -1.0, 1.0, ALU.mult, ALU.add).then_inc(c_ready, 1)
                dve.wait_ge(c_ready, ITERS + 3)
                dve.tensor_tensor(s16[:, :], s16[:, :], m16[:, :], ALU.add).then_inc(sel16_ready, 1)

            def sums_out_pre(g):
                for j in range(4):
                    xt = x_all[:, bass.ds(4 * g + j, 1), :].rearrange("p a d -> p (a d)")
                    last = dve.tensor_tensor(xt, xt, row_b[:, 1, :], ALU.add)
                last.then_inc(x_biased, 1)
                dve.wait_ge(x_biased, g + 1)

            z_tiles(0)
            dve.wait_ge(s16_ps, 1)
            dve.tensor_scalar(e16[:, :], bank[3][0:B, 0:N], 0.0, None, ALU.min).then_inc(descent_v, 1)
            dve.wait_ge(descent_v, TILES + 3)
            dve.tensor_reduce(cc[:, 1:2], e16[:, :], AX_X, ALU.max).then_inc(descent_v, 1)
            dve.wait_ge(descent_v, TILES + 4)
            dve.tensor_scalar(e16[:, :], e16[:, :], cc[:, 1:2], None, ALU.subtract).then_inc(e_ready, 1)
            zT_low(0)
            dve.wait_ge(exp_ready, 1)
            ffn(0, first=True)
            dve.wait_ge(sel_ps, 1)
            dve.tensor_copy(sel[:, :, :].rearrange("p j b -> p (j b)"), bank[4][:, 0:TT * B]).then_inc(sel_ready, 1)
            dve.wait_ge(sel_ready, 1)
            with dve.Fori(1, PAIRS - 1) as g:
                ffn(g)
            ffn(PAIRS - 1, more=False)
            final(PAIRS - 1)

        @block.scalar
        def _(act):
            act.wait_ge(consts_in, 16 * 5)

            def front_out(f, first=False):
                act.wait_ge(ps["lnT"], f + 1)
                if not first:
                    act.wait_ge(lnT_lo_ready, f)
                for k in range(2):
                    last = act.activation(lnT[:, k, :], kind_bank["lnT"][:, k * N:(k + 1) * N], ACT.Identity,
                                          bias=vk[:, 2 + k:3 + k], scale=vk[:, k:k + 1])
                last.then_inc(rd["lnT"], 1)
                act.wait_ge(ps["cT"], f + 1)
                if not first:
                    act.wait_ge(cT_lo_ready, f)
                    act.wait_ge(cT_stacked, f)
                for k in range(2):
                    last = act.activation(cT[:, k, :], kind_bank["cT"][:, k * N:(k + 1) * N], ACT.Identity,
                                          bias=vc[:, 2 + k:3 + k], scale=vc[:, k:k + 1])
                last.then_inc(rd["cT"], 1)

            def projections_out(f, fp, first=False):
                for j in range(TT):
                    act.wait_ge(ps[f"qk{j}"], f + 1)
                    if j == 0 and not first:
                        act.wait_ge(ps["kT1"], f)
                        act.wait_ge(ss_ctx, f)
                    act.copy(qk[:, j, :], kind_bank[f"qk{j}"][:, :])
                    act.activation(sq[:, 2 * j:2 * j + 2, :].rearrange("p a d -> p (a d)"), kind_bank[f"qk{j}"][:, :],
                                   ACT.Square).then_inc(rd[f"qk{j}"], 1)
                for j in range(TT):
                    act.wait_ge(ps[f"kv{j}"], f + 1)
                    act.copy(kc[:, j, :], kind_bank[f"kv{j}"][:, 0:D])
                    act.activation(sq[:, 4 + j, :], kind_bank[f"kv{j}"][:, 0:D], ACT.Square)
                    act.copy(v_aug[fp][:, TT + j, :, 0:DH],
                             kind_bank[f"kv{j}"][:, D:2 * D].rearrange("p (h d) -> p h d", h=HEADS)
                             ).then_inc(rd[f"kv{j}"], 1)

            def exponentials(t, qt):
                for h in range(HEADS):
                    u = qt * HEADS + h
                    act.wait_ge(s_masked, 8 * t + u + 3)
                    act.activation(prob[:, u, :], prob[:, u, :], ACT.Exp, bias=mn[:, u:u + 1], scale=-1.0
                                   ).then_inc(p_ready, 1)

            def probT_odd(t, u):
                act.wait_ge(pt_ps, 8 * t + u + 1)
                if u >= 4:
                    act.wait_ge(pv_done, 8 * t + u - 3)
                act.copy(probT[:, u % 4, :, :].rearrange("p k q -> p (k q)"), pt_bank[1][:, :]).then_inc(pt_odd, 1)

            act.copy(cred[:, 0:1], vk[:, 0:1]).then_inc(pt_odd, 1)
            front_out(0, first=True)
            projections_out(0, 0, first=True)

            def step(t, p):
                f = t + 1
                exponentials(t, 0)
                front_out(f)
                exponentials(t, 1)
                projections_out(f, 1 - p)
                for u in (1, 3, 5, 7):
                    probT_odd(t, u)

            with act.Fori(0, (B - 2) // 2) as i:
                step(2 * i, 0)
                step(2 * i + 1, 1)
            step(B - 2, 0)
            exponentials(B - 1, 0)
            exponentials(B - 1, 1)
            for u in (1, 3, 5, 7):
                probT_odd(B - 1, u)

            act.wait_ge(e_ready, 1)
            act.activation(e16[:, :], e16[:, :], ACT.Exp).then_inc(exp_ready, 1)
            act.copy(cred[:, 1:2], vk[:, 0:1]).then_inc(gelu_done, 3)

            def zT_high(g):
                for kt in range(2):
                    act.wait_ge(zT_ps, 2 * g + kt + 1)
                    act.copy(zT_hi[:, kt, :], bank[7][:, :]).then_inc(zT_hi_s, 1)

            def gelu(g, m, early):
                act.wait_ge(h_ps, HT * g + m + 1)
                if not early:
                    act.wait_ge(h_lo_s, HT * g + m - 2)
                act.activation(h_raw[m % 3], bank[4 + m % 3][:, :], ACT.Gelu, bias=vh[:, 4 + m:5 + m]
                               ).then_inc(gelu_done, 1)
                act.wait_ge(gelu_done, HT * g + m + 4)
                if not early:
                    act.wait_ge(h_used, HT * g + m - 2)
                act.copy(h_hi[m % 3][:, :], h_raw[m % 3]).then_inc(h_hi_s, 1)

            def ffn(g, first=False, more=True):
                for m in range(HT):
                    gelu(g, m, first and m < 3)
                if more:
                    zT_high(g + 1)

            zT_high(0)
            ffn(0, first=True)
            with act.Fori(1, PAIRS - 1) as g:
                ffn(g)
            ffn(PAIRS - 1, more=False)

        @block.gpsimd
        def _(pool):
            pool.dma_start(vk[:, :], vec_k).then_inc(consts_in, 16)
            pool.dma_start(vc[:, :], vec_c).then_inc(consts_in, 16)
            pool.dma_start(vh[:, :], vec_h).then_inc(consts_in, 16)
            pool.dma_start(ident[:, :], eye).then_inc(consts_in, 16)
            pool.dma_start(row_b[:, :, :], rows.rearrange("(o r) d -> o r d", o=1).broadcast_to([P, 4, D])
                           ).then_inc(consts_in, 16)
            pool.memset(neg_half[:, :], -0.5).then_inc(setup_p, 1)
            pool.memset(maskb[0][:, :], 0.0).then_inc(setup_p, 1)
            pool.memset(maskb[1][:, :], 0.0).then_inc(setup_p, 1)
            pool.wait_ge(setup_p, 3)

            def inverse_std(b):
                pool.wait_ge(mv_ready, b + 1)
                pool.sem_inc(turn_p)
                v = mv[:, :, 1:2].rearrange("p t o -> p (t o)")
                pool.tensor_scalar(rstd[:, 0:TT], v[:, 0:TT], 1.0 + LN_EPS, LN_EPS * LN_EPS, ALU.mult, ALU.add)
                pool.tensor_scalar(rstd[:, TT:4], v[:, TT:4], 1.0, LN_EPS, ALU.mult, ALU.add).then_inc(pool_step, 1)
                pool.wait_ge(pool_step, b + 1)
                pool.tensor_tensor(rstd[:, :], rstd[:, :], neg_half[:, 0:4], ALU.pow).then_inc(rstd_ready, 1)

            def low_parts(f):
                pool.wait_ge(lnT_hi_ready, f + 1)
                pool.tensor_tensor(lnT_lo[:, :, :], lnT[:, :, :], lnT_hi[:, :, :].bitcast(F32), ALU.subtract
                                   ).then_inc(lnT_lo_ready, 1)
                pool.wait_ge(cT_hi_ready, f + 1)
                pool.tensor_tensor(cT_lo[:, :], cT[:, 0, :], cT_hi[:, 0, :].bitcast(F32), ALU.subtract
                                   ).then_inc(cT_lo_ready, 1)

            def mask_bias(b, p):
                pool.tensor_copy(maskb[p][:, N:KEYS], mask_all[:, bass.ds(b * N, N)]).then_inc(pool_step2, 1)
                pool.wait_ge(pool_step2, b + 1)
                pool.sem_inc(turn_p)
                pool.tensor_scalar(maskb[p][:, N:KEYS], maskb[p][:, N:KEYS], -1.0, -BIG, ALU.add, ALU.mult
                                   ).then_inc(mask_ready, 1)

            def add_bo(b):
                pool.wait_ge(ln_ready, b + 1)
                xt = x_all[:, bass.ds(2 * b, TT), :]
                pool.tensor_tensor(xt, xt, row_b[:, 0:1, :].broadcast_to([P, TT, D]), ALU.add).then_inc(xbo_ready, 1)

            def inverse_norms(f, lat):
                c = slice(0, 16) if lat else slice(16, 24)
                pool.wait_ge(ss_lat if lat else ss_ctx, f + 1)
                pool.sem_inc(turn_p)
                pool.tensor_scalar(ss[:, c], ss[:, c], 1.0 / DH, 1e-16, ALU.mult, ALU.max).then_inc(norm_step, 1)
                pool.wait_ge(norm_step, 2 * f + (1 if lat else 2))
                pool.tensor_tensor(rr[:, c], ss[:, c], neg_half[:, c], ALU.pow).then_inc(rr_lat if lat else rr_ctx, 1)

            def scale_ctx(f):
                pool.wait_ge(rr_ctx, f + 1)
                v = kc[:, :, :].rearrange("p j (h d) -> p (j h) d", d=DH)
                pool.tensor_tensor(v, v, rr[:, 16:24].rearrange("p (h o) -> p h o", o=1).broadcast_to([P, 8, DH]),
                                   ALU.mult).then_inc(ctx_scaled, 1)

            def front(f, fp):
                low_parts(f)
                mask_bias(f, fp)
                add_bo(f)
                inverse_norms(f, True)
                inverse_norms(f, False)
                scale_ctx(f)

            pool.wait_ge(mask_in, 16)
            pool.wait_ge(consts_in, 16 * 5)
            inverse_std(0)
            front(0, 0)
            inverse_std(1)
            with pool.Fori(0, (B - 2) // 2) as i:
                for p in range(2):
                    front(2 * i + p + 1, 1 - p)
                    inverse_std(2 * i + p + 2)
            front(B - 1, 1)

            def chain(ins):
                steps[0] += 1
                ins.then_inc(tail_step, 1)
                pool.wait_ge(tail_step, steps[0])

            steps = [0]
            pool.wait_ge(x2_stats, 1)
            var = stats2[:, :, 1:2].rearrange("p t o -> p (t o)")
            chain(pool.tensor_scalar(r2[:, :], var, 1.0, LN_EPS, ALU.mult, ALU.add))
            chain(pool.tensor_tensor(r2[:, :], r2[:, :], neg_half[:, :], ALU.pow))
            chain(pool.tensor_tensor(zs[:, :], r2[:, :], r2[:, :], ALU.mult))
            chain(pool.tensor_tensor(zs[:, :], zs[:, :], var, ALU.mult))
            chain(pool.tensor_scalar(zs[:, :], zs[:, :], 1.0, 1e-24 / D, ALU.mult, ALU.max))
            chain(pool.tensor_tensor(zs[:, :], zs[:, :], neg_half[:, :], ALU.pow))
            pool.tensor_tensor(zs[:, :], zs[:, :], r2[:, :], ALU.mult).then_inc(zs_ready, 1)


def kernel(**inputs):
    import concourse.bacc as bacc
    from concourse.bass_utils import run_bass_kernel_spmd

    def get(name):
        return np.asarray(inputs[name])

    def cols(v):
        return np.ascontiguousarray(v.reshape(-1, P).T)

    def pre(name):
        return get("L0_ffn_" + name)

    w_lat = np.concatenate([get("L0_xattn_Wq").T, get("L0_xattn_Wlkv").T], axis=1)
    w_ctx = get("L0_xattn_Wkv").T
    w_ctx = np.concatenate([w_ctx, w_ctx[P:DC]], axis=0)

    def ctx_vec(v):
        return cols(np.concatenate([v, v[P:DC]]))

    def head_vec(v):
        return np.concatenate([v, v])[:, None]

    arrays = {
        "x": get("x"),
        "ctx_in": get("ctx_768"),
        "mask": get("mask_BxS2_bk0"),
        "w_lat": w_lat,
        "w_ctx": w_ctx,
        "w_o": get("L0_xattn_Wo").T,
        "w1": np.concatenate([pre("light_w1"), pre("heavy_w1")], axis=1),
        "w2": np.concatenate([pre("light_w2"), pre("heavy_w2")], axis=0),
        "vec_k": np.concatenate([cols(get("L0_xattn_ln_l_g")), cols(get("L0_xattn_ln_l_b")),
                                 head_vec(get("L0_xattn_qn_g")), head_vec(get("L0_xattn_kn_g"))], axis=1),
        "vec_c": np.concatenate([ctx_vec(get("L0_xattn_ln_x_g")), ctx_vec(get("L0_xattn_ln_x_b"))], axis=1),
        "vec_h": np.concatenate([cols(pre("light_gamma")), cols(pre("heavy_gamma")),
                                 cols(pre("light_b1")), cols(pre("heavy_b1"))], axis=1),
        "rows": np.stack([get("L0_xattn_bo"), pre("light_b2"), pre("heavy_b2"), pre("routing_token")]),
        "eye": np.eye(P, dtype=np.float32),
    }
    arrays = {k: np.ascontiguousarray(v) for k, v in arrays.items()}
    nc = bacc.Bacc("TRN2", target_bir_lowering=False, num_devices=1)
    aps = [nc.dram_tensor("in_" + k, v.shape, mybir.dt.from_np(v.dtype), kind="ExternalInput").ap()
           for k, v in arrays.items()]
    out = nc.dram_tensor("out_0", (B, N, D), F32, kind="ExternalOutput").ap()
    build(nc, *aps, out)
    r = run_bass_kernel_spmd(nc, [{"in_" + k: v for k, v in arrays.items()}], core_ids=[0])
    return r.results[0]["out_0"]
```

```python
from contextlib import ExitStack

import numpy as np

import concourse.bass as bass
from concourse import mybir

ALU = mybir.AluOpType
ACT = mybir.ActivationFunctionType
F32 = mybir.dt.float32
F32R = mybir.dt.float32r
U8 = mybir.dt.uint8
AX_X = mybir.AxisListType.X

P = 128
B = 16
N = 256
D = 256
DC = 192
HEADS = 4
DH = 64
KEYS = 2 * N
TT = N // P
KT = KEYS // P
TILES = B * TT
PAIRS = B // 2
HID_L = 128
HID_H = 1024
HT = (HID_L + HID_H) // P
ITERS = 50
LN_EPS = 1e-5
BIG = 3.0e38


def build(nc, x, ctx_in, mask, w_lat, w_ctx, w_o, w1, w2, vecs, rows, out):
    ctx = ExitStack()
    with ctx:
        def sb(name, shape, dt=F32):
            return ctx.enter_context(nc.sbuf_tensor(name, shape, dt))

        def sem(name):
            return ctx.enter_context(nc.semaphore(name))

        bank = [ctx.enter_context(nc.psum_tensor(f"bank{i}", [P, 512], F32)) for i in range(8)]

        x_all = sb("x_all", [P, TILES, D])
        wlat_hi = sb("wlat_hi", [P, 2, 3 * D], F32R)
        wlat_lo = sb("wlat_lo", [P, 2, 3 * D], F32R)
        wctx_hi = sb("wctx_hi", [P, 2, 2 * D], F32R)
        wctx_lo = sb("wctx_lo", [P, 2, 2 * D], F32R)
        wo = sb("wo", [P, 2, D])
        w1_hi = sb("w1_hi", [P, 2, HT * P], F32R)
        w1_lo = sb("w1_lo", [P, 2, HT * P], F32R)
        w2_hi = sb("w2_hi", [P, HT, D], F32R)
        w2_lo = sb("w2_lo", [P, HT, D], F32R)
        vecs_sb = sb("vecs_sb", [P, 14 + HT + P])
        row_b = sb("row_b", [P, 4, D])
        neg_half = sb("neg_half", [P, 32])
        neg_gqk = sb("neg_gqk", [P, 1])
        rt_sum = sb("rt_sum", [P, 1])
        mean2 = sb("mean2", [P, TILES])
        zr = sb("zr", [P, B, 2, TT])
        x2 = sb("x2", [P, TT, D])
        st6b = sb("st6b", [P, TT, 6])
        mv2 = sb("mv2", [P, TT, 2])
        dot2 = sb("dot2", [P, TT])
        dots = sb("dots", [P, TILES])
        mask_all = sb("mask_all", [P, B * N], U8)

        c_in = [sb(f"c_in{p}", [P, TT, DC]) for p in range(2)]
        st6 = sb("st6", [P, 4, 6])
        mv = sb("mv", [P, 4, 2])
        rstd = sb("rstd", [P, 4])
        ln = sb("ln", [P, TT, D])
        cn = sb("cn", [P, TT, DC + 64])
        lnT = sb("lnT", [P, 2, N])
        lnT_hi = sb("lnT_hi", [P, 2, N], F32R)
        lnT_lo = sb("lnT_lo", [P, 2, N], F32R)
        cT = sb("cT", [P, 2, N])
        cT_hi = sb("cT_hi", [P, 2, N], F32R)
        cT_lo = sb("cT_lo", [P, N], F32R)
        qk = sb("qk", [P, TT, 2 * D])
        kc = sb("kc", [P, TT, D])
        sq = sb("sq", [P, 6, D])
        ss = sb("ss", [P, 6 * HEADS])
        rr = sb("rr", [P, 6 * HEADS])
        v_aug = [sb(f"v_aug{p}", [P, KT, HEADS, DH + 1]) for p in range(2)]
        qT = sb("qT", [P, 2, N])
        kT = sb("kT", [P, 2, KEYS])
        maskb = [sb(f"maskb{p}", [P, KEYS]) for p in range(2)]
        prob = sb("prob", [P, TT * HEADS, KEYS])
        mn = sb("mn", [P, TT * HEADS])
        probT = sb("probT", [P, 4, KT, P])
        rden = sb("rden", [P, HEADS])
        vtmp = sb("vtmp", [P, 2, TT])
        o_n = sb("o_n", [P, TT, D])
        o_T = sb("o_T", [P, 2, N])

        z = qk[:, :, :].rearrange("p a b -> p (a b)").rearrange("p (j d) -> p j d", j=4)
        zT_hi = sb("zT_hi", [P, 2, 512], F32R)
        zT_lo = sb("zT_lo", [P, 2, 512], F32R)
        h_raw = [prob[:, 2 + i, :] for i in range(3)]
        h_hi = [sb(f"h_hi{i}", [P, 512], F32R) for i in range(3)]
        h_lo = [sb(f"h_lo{i}", [P, 512], F32R) for i in range(3)]
        probT_flat = probT[:, :, :, :].rearrange("p a b c -> p (a b c)")
        hv = [probT_flat[:, i * 4 * D:(i + 1) * 4 * D].rearrange("p (a d) -> p a d", a=4) for i in range(2)]
        hv.append(sq[:, 0:4, :])
        sm = sb("sm", [P, TILES])
        s_tok = sb("s_tok", [P, TILES])
        cred = sb("cred", [P, 3])
        s16 = sb("s16", [B, N])
        e16 = sb("e16", [B, N])
        m16 = sb("m16", [B, N])
        cc = sb("cc", [B, 4])
        sel = sb("sel", [P, TT, B])

        vk = vecs_sb[:, 0:6]
        vc = vecs_sb[:, 6:10]
        vh = vecs_sb[:, 10:14 + HT]
        ident = vecs_sb[:, 14 + HT:14 + HT + P]

        wctx_raw = prob[:, 5:7, :].rearrange("p a b -> p (a b)").rearrange("p (k n) -> p k n", k=2)
        wlat_raw = sq[:, :, :].rearrange("p a b -> p (a b)").rearrange("p (k n) -> p k n", k=2)
        w1_raw = x_all[:, TILES - 2 * HT:TILES - HT, :].rearrange("p a b -> p (a b)").rearrange("p (k n) -> p k n", k=2)
        w2_raw = x_all[:, TILES - HT:TILES, :]

        vecs_in, rows_in = sem("vecs_in"), sem("rows_in")
        wlat_in, wctx_in, w1_in, w2_in, wo_in, mask_in = (sem(s) for s in (
            "wlat_in", "wctx_in", "w1_in", "w2_in", "wo_in", "mask_in"))
        batch_in = [sem(f"batch_in{p}") for p in range(2)]
        out_done = sem("out_done")
        setup_v, setup_p = sem("setup_v"), sem("setup_p")
        wlat_hi_s, wctx_hi_s, wlat_lo_s, wctx_lo_s = (sem(s) for s in (
            "wlat_hi_s", "wctx_hi_s", "wlat_lo_s", "wctx_lo_s"))
        w1_scaled, w_hi_s, w_lo_s = sem("w1_scaled"), sem("w_hi_s"), sem("w_lo_s")
        kinds = ("qk0", "qk1", "v01", "kv0", "kv1", "lnT", "cT", "qT", "kT0", "oT", "kT1", "y")
        ps = {k: sem(k + "_ps") for k in kinds}
        rd = {k: sem(k + "_sb") for k in kinds}
        mv_ready, rstd_ready, ln_ready, small_v = sem("mv_ready"), sem("rstd_ready"), sem("ln_ready"), sem("small_v")
        pool_step, pool_step2 = sem("pool_step"), sem("pool_step2")
        lnT_hi_ready, lnT_lo_ready = sem("lnT_hi_ready"), sem("lnT_lo_ready")
        cT_hi_ready, cT_stacked, cT_lo_ready = sem("cT_hi_ready"), sem("cT_stacked"), sem("cT_lo_ready")
        ss_lat, ss_ctx, rr_lat, rr_ctx = sem("ss_lat"), sem("ss_ctx"), sem("rr_lat"), sem("rr_ctx")
        lat_scaled, ctx_scaled = sem("lat_scaled"), sem("ctx_scaled")
        mask_ready, xbo_ready = sem("mask_ready"), sem("xbo_ready")
        s_ps, s_masked, p_ready = sem("s_ps"), sem("s_masked"), sem("p_ready")
        pt_ps = sem("pt_ps")
        pt_even, pt_odd = sem("pt_even"), sem("pt_odd")
        pv_done, o_rcp, o_sb = sem("pv_done"), sem("o_rcp"), sem("o_sb")
        x2_read, mv2_ready, x2_stats, x2_kept, zr_ready, zr_step = (sem(k) for k in (
            "x2_read", "mv2_ready", "x2_stats", "x2_kept", "zr_ready", "zr_step"))
        s_ready, s16_ps, s16_read, e_ready, exp_ready, sel16_ready, sel_ps, sel_ready = (sem(s) for s in (
            "s_ready", "s16_ps", "s16_read", "e_ready", "exp_ready", "sel16_ready", "sel_ps", "sel_ready"))
        descent_v, c_sum, c_ready = sem("descent_v"), sem("c_sum"), sem("c_ready")
        turn_v, turn_p = sem("turn_v"), sem("turn_p")
        x_biased, norm_step = sem("x_biased"), sem("norm_step")
        z_ready, zT_ps, zT_hi_s, zT_lo_s = sem("z_ready"), sem("zT_ps"), sem("zT_hi_s"), sem("zT_lo_s")
        h_ps, gelu_done, h_hi_s, h_lo_s, h_used, acc_sb, fin = (sem(s) for s in (
            "h_ps", "gelu_done", "h_hi_s", "h_lo_s", "h_used", "acc_sb", "fin"))

        kind_bank = {k: bank[i % 3] for i, k in enumerate(kinds)}
        s_bank = [bank[3], bank[4]]
        pt_bank = [bank[5], bank[6]]
        o_bank = bank[7]

        x_t = x.rearrange("b (j p) d -> p (b j) d", p=P)
        out_t = out.rearrange("b (j p) d -> p (b j) d", p=P)
        c_t = ctx_in.rearrange("b (j p) d -> p (b j) d", p=P)

        block = ctx.enter_context(nc.Block())

        @block.sync
        def _(sp):
            def load(b, p):
                sp.dma_start(x_all[:, bass.ds(2 * b, TT), :], x_t[:, bass.ds(2 * b, TT), :]).then_inc(batch_in[p], 16)
                sp.dma_start(c_in[p][:, :, :], c_t[:, bass.ds(2 * b, TT), :]).then_inc(batch_in[p], 16)

            load(0, 0)
            sp.dma_start(wlat_raw, w_lat.rearrange("(k p) n -> p k n", p=P)).then_inc(wlat_in, 16)
            sp.dma_start(wctx_raw, w_ctx.rearrange("(k p) n -> p k n", p=P)).then_inc(wctx_in, 16)
            load(1, 1)
            sp.dma_start(mask_all[:, :], mask.rearrange("(o b) n -> o (b n)", o=1).broadcast_to([P, B * N])).then_inc(mask_in, 16)
            sp.dma_start(wo[:, :, :], w_o.rearrange("(k p) n -> p k n", p=P)).then_inc(wo_in, 16)
            sp.dma_start(w1_raw, w1.rearrange("(k p) n -> p k n", p=P)).then_inc(w1_in, 16)
            sp.dma_start(w2_raw, w2.rearrange("(k p) n -> p k n", p=P)).then_inc(w2_in, 16)
            def load_pairs(lo, hi):
                with sp.Fori(lo, hi) as i:
                    for p in range(2):
                        sp.wait_ge(ln_ready, 2 * i + p - 1)
                        load(2 * i + p, p)

            weights_from = (TILES - 2 * HT) // TT
            load_pairs(1, weights_from // 2)
            sp.wait_ge(w_lo_s, 6)
            load_pairs(weights_from // 2, B // 2)
            with sp.Fori(0, PAIRS) as g:
                sp.wait_ge(fin, g + 1)
                sp.dma_start(out_t[:, bass.ds(4 * g, 4), :], x_all[:, bass.ds(4 * g, 4), :]).then_inc(out_done, 16)
            sp.wait_ge(out_done, 16 * PAIRS)

        @block.tensor
        def _(pe):
            def take(kind, need):
                if need is not None:
                    pe.wait_ge(rd[need[0]], need[1])

            def split_products(dst, pairs):
                for n, (shi, slo, mhi, mlo) in enumerate(pairs):
                    terms = [(shi, mhi), (shi, mlo)] + ([(slo, mhi)] if slo is not None else [])
                    for m, (s, v) in enumerate(terms):
                        last = pe.matmul(dst, s, v, start=(n == 0 and m == 0),
                                         stop=(n == len(pairs) - 1 and m == len(terms) - 1))
                return last

            def front_transposes(f, need_ln, need_c):
                pe.wait_ge(ln_ready, f + 1)
                take("lnT", need_ln)
                for kt in range(2):
                    for j in range(TT):
                        last = pe.transpose(kind_bank["lnT"][:, kt * N + j * P:kt * N + (j + 1) * P],
                                            ln[:, j, kt * P:(kt + 1) * P], ident[:, :])
                last.then_inc(ps["lnT"], 1)
                take("cT", need_c)
                for kt in range(2):
                    for j in range(TT):
                        last = pe.transpose(kind_bank["cT"][:, kt * N + j * P:kt * N + (j + 1) * P],
                                            cn[:, j, kt * P:(kt + 1) * P], ident[:, :])
                last.then_inc(ps["cT"], 1)

            def lat_pairs(j, c0, c1):
                t = slice(j * P, (j + 1) * P)
                return [(lnT_hi[:, kt, t], lnT_lo[:, kt, t], wlat_hi[:, kt, c0:c1], wlat_lo[:, kt, c0:c1])
                        for kt in range(2)]

            def project_qk(f, j, need):
                if j == 0:
                    pe.wait_ge(lnT_hi_ready, f + 1)
                    pe.wait_ge(lnT_lo_ready, f + 1)
                take(f"qk{j}", need)
                split_products(kind_bank[f"qk{j}"][:, :], lat_pairs(j, 0, 2 * D)).then_inc(ps[f"qk{j}"], 1)

            def project_v(f, need):
                take("v01", need)
                for j in range(TT):
                    last = split_products(kind_bank["v01"][:, j * D:(j + 1) * D], lat_pairs(j, 2 * D, 3 * D))
                last.then_inc(ps["v01"], 1)

            def project_ctx(f):
                pe.wait_ge(cT_stacked, f + 1)
                pe.wait_ge(cT_lo_ready, f + 1)
                for j in range(TT):
                    take(f"kv{j}", (f"qk{j}", f + 1))
                    t = slice(j * P, (j + 1) * P)
                    dst = kind_bank[f"kv{j}"][:, :]
                    pe.matmul(dst, cT_hi[:, 1, t], wctx_hi[:, 1, :], start=True, stop=False)
                    pe.matmul(dst, cT_hi[0:DH, 1, t], wctx_lo[0:DH, 1, :], start=False, stop=False)
                    pe.matmul(dst, cT_hi[:, 0, t], wctx_hi[:, 0, :], start=False, stop=False)
                    pe.matmul(dst, cT_hi[:, 0, t], wctx_lo[:, 0, :], start=False, stop=False)
                    pe.matmul(dst, cT_lo[:, t], wctx_hi[:, 0, :], start=False, stop=True).then_inc(ps[f"kv{j}"], 1)

            def q_transposes(f):
                pe.wait_ge(lat_scaled, f + 1)
                take("qT", ("kv1", f + 1))
                for c in range(2):
                    for j in range(TT):
                        last = pe.transpose(kind_bank["qT"][:, c * N + j * P:c * N + (j + 1) * P],
                                            qk[:, j, c * P:(c + 1) * P], ident[:, :])
                last.then_inc(ps["qT"], 1)

            def k_transposes(f, c, need):
                if c == 0:
                    pe.wait_ge(ctx_scaled, f + 1)
                take(f"kT{c}", need)
                for t in range(KT):
                    src = qk[:, t, D + c * P:D + (c + 1) * P] if t < TT else kc[:, t - TT, c * P:(c + 1) * P]
                    last = pe.transpose(kind_bank[f"kT{c}"][:, t * P:(t + 1) * P], src, ident[:, :])
                last.then_inc(ps[f"kT{c}"], 1)

            def scores(t, u0):
                if u0 == 0:
                    for k in ("qT", "kT0", "kT1"):
                        pe.wait_ge(rd[k], t + 1)
                for u in (u0, u0 + 1):
                    qt, h = divmod(u, HEADS)
                    pe.wait_ge(s_masked, 8 * t + u + 1)
                    r = slice(DH * (h % 2), DH * (h % 2) + DH)
                    pe.matmul(s_bank[h % 2][:, :], qT[r, h // 2, qt * P:(qt + 1) * P], kT[r, h // 2, :],
                              start=True, stop=True).then_inc(s_ps, 1)

            def prob_transposes(t, u):
                pe.wait_ge(p_ready, 8 * t + u + 1)
                pe.wait_ge(pt_even if u % 2 == 0 else pt_odd, 4 * t + u // 2 + 1)
                for k in range(KT):
                    last = pe.transpose(pt_bank[u % 2][:, k * P:(k + 1) * P], prob[:, u, k * P:(k + 1) * P], ident[:, :])
                last.then_inc(pt_ps, 1)

            def weighted_values(t, u, p):
                qt, h = divmod(u, HEADS)
                pe.wait_ge(pt_even if u % 2 == 0 else pt_odd, 4 * t + u // 2 + 2)
                if u == 0:
                    pe.wait_ge(rd["v01"], t + 1)
                    pe.wait_ge(rd["kv1"], t + 1)
                if h == 0:
                    pe.wait_ge(o_sb, 2 * t + qt + 1)
                for k in range(KT):
                    last = pe.matmul(o_bank[:, h * (DH + 1):(h + 1) * (DH + 1)], probT[:, u % 4, k, :],
                                     v_aug[p][:, k, h, :], start=(k == 0), stop=(k == KT - 1))
                last.then_inc(pv_done, 1)

            def attend(t, p, units):
                for u in units:
                    if u < 8:
                        prob_transposes(t, u)
                    weighted_values(t, u - 1, p)

            def o_transposes(t, need):
                pe.wait_ge(o_sb, 2 * t + 3)
                take("oT", need)
                for c in range(2):
                    for j in range(TT):
                        last = pe.transpose(kind_bank["oT"][:, c * N + j * P:c * N + (j + 1) * P],
                                            o_n[:, j, c * P:(c + 1) * P], ident[:, :])
                last.then_inc(ps["oT"], 1)

            def out_projection(t, need):
                pe.wait_ge(rd["oT"], t + 2)
                take("y", need)
                for j in range(TT):
                    for c in range(2):
                        last = pe.matmul(kind_bank["y"][:, j * D:(j + 1) * D], o_T[:, c, j * P:(j + 1) * P],
                                         wo[:, c, :], start=(c == 0), stop=(c == 1))
                last.then_inc(ps["y"], 1)

            pe.wait_ge(vecs_in, 16)
            front_transposes(0, None, None)
            pe.wait_ge(wlat_lo_s, 1)
            project_qk(0, 0, ("cT", 1))
            project_qk(0, 1, None)
            project_v(0, ("lnT", 1))
            pe.wait_ge(wctx_lo_s, 1)
            project_ctx(0)
            front_transposes(1, ("v01", 1), ("kv0", 1))
            q_transposes(0)
            k_transposes(0, 0, ("lnT", 2))
            k_transposes(0, 1, ("qT", 1))
            pe.wait_ge(wo_in, 16)

            def step(t, p, more=True):
                f, n = t + 1, t + 2
                scores(t, 0)
                project_qk(f, 0, ("oT", t + 1))
                scores(t, 2)
                project_qk(f, 1, ("kT1", t + 1))
                scores(t, 4)
                scores(t, 6)
                prob_transposes(t, 0)
                project_ctx(f)
                attend(t, p, range(1, 5))
                prob_transposes(t, 5)
                project_v(f, ("y", t + 1))
                weighted_values(t, 4, p)
                attend(t, p, (6, 7))
                if more:
                    front_transposes(n, ("v01", f + 1), ("kv0", f + 1))
                attend(t, p, (8,))
                q_transposes(f)
                k_transposes(f, 0, ("lnT", n + 1) if more else ("v01", f + 1))
                o_transposes(t, ("cT", n + 1) if more else ("kv0", f + 1))
                k_transposes(f, 1, ("qT", f + 1))
                out_projection(t, ("kT0", f + 1))

            with pe.Fori(0, (B - 2) // 2) as i:
                step(2 * i, 0)
                step(2 * i + 1, 1)
            step(B - 2, 0, more=False)
            for u in range(0, 8, 2):
                scores(B - 1, u)

            acc = bank[0:4]
            h_bank = bank[4:7]

            def z_transposes(g, kt, first=False):
                pe.wait_ge(z_ready, g + 1)
                if not first:
                    pe.wait_ge(zT_lo_s, 2 * g + kt + 1)
                dst = bank[1 + kt] if first else bank[7]
                for j in range(4):
                    last = pe.transpose(dst[:, j * P:(j + 1) * P], z[:, j, kt * P:(kt + 1) * P], ident[:, :])
                last.then_inc(zT_ps, 1)

            def hidden(g, m):
                pe.wait_ge(gelu_done, HT * g + m + 1)
                t = slice(m * P, (m + 1) * P)
                for k in range(2):
                    if m == 0:
                        pe.wait_ge(zT_hi_s, 2 * g + k + 1)
                        pe.wait_ge(zT_lo_s, 2 * g + k + 2)
                    for n, (w, v) in enumerate(((w1_hi, zT_hi), (w1_hi, zT_lo), (w1_lo, zT_hi))):
                        last = pe.matmul(h_bank[m % 3][:, :], w[:, k, t], v[:, k, :],
                                         start=(k == 0 and n == 0), stop=(k == 1 and n == 2))
                last.then_inc(h_ps, 1)

            def outputs(g, m):
                pe.wait_ge(h_hi_s, HT * g + m + 1)
                pe.wait_ge(h_lo_s, HT * g + m + 1)
                if m == 0:
                    pe.wait_ge(acc_sb, g + 1)
                c = slice(0, D) if m == 0 else slice(D, 2 * D)
                for j in range(4):
                    t = slice(j * P, (j + 1) * P)
                    terms = ((h_hi[m % 3][:, t], w2_hi[:, m, :]), (h_hi[m % 3][:, t], w2_lo[:, m, :]),
                             (h_lo[m % 3][:, t], w2_hi[:, m, :]))
                    for n, (s, v) in enumerate(terms):
                        last = pe.matmul(acc[j][:, c], s, v, start=(m <= 1 and n == 0),
                                         stop=(m in (0, HT - 1) and n == 2))
                last.then_inc(h_used, 1)

            def score_transposes():
                pe.wait_ge(s_ready, 1)
                for j in range(TT):
                    last = pe.transpose(bank[7][0:B, j * P:(j + 1) * P], s_tok[:, j:TILES:TT], ident[:, :])
                last.then_inc(s16_ps, 1)

            def selection_transposes():
                pe.wait_ge(sel16_ready, 1)
                for j in range(TT):
                    last = pe.transpose(bank[7][:, j * B:(j + 1) * B], s16[:, j * P:(j + 1) * P], ident[0:B, 0:B])
                last.then_inc(sel_ps, 1)

            def ffn(g, first=False, more=True, select=False):
                if not first:
                    hidden(g, 0)
                    hidden(g, 1)
                for m in range(HT):
                    if m + 2 < HT:
                        hidden(g, m + 2)
                    if first and m == 3:
                        score_transposes()
                    if first and m == 0:
                        pe.wait_ge(rd["y"], B + 1)
                    if select and m == 2:
                        selection_transposes()
                    if more and m == HT - 3:
                        if first:
                            pe.wait_ge(s16_read, 1)
                        if select:
                            pe.wait_ge(sel_ready, 1)
                        z_transposes(g + 1, 0)
                    if more and m == HT - 1:
                        z_transposes(g + 1, 1)
                    outputs(g, m)

            prob_transposes(B - 1, 0)
            attend(B - 1, 1, range(1, 4))
            pe.wait_ge(rd["y"], B)
            for kt in range(2):
                z_transposes(0, kt, first=True)
            attend(B - 1, 1, range(4, 9))
            pe.wait_ge(w_lo_s, 6)
            hidden(0, 0)
            o_transposes(B - 1, None)
            hidden(0, 1)
            out_projection(B - 1, ("y", B))
            ffn(0, first=True)
            with pe.Fori(1, 3) as g:
                ffn(g)
            ffn(3, select=True)
            with pe.Fori(4, PAIRS - 1) as g:
                ffn(g)
            ffn(PAIRS - 1, more=False)

        @block.vector
        def _(dve):
            dve.memset(v_aug[0][:, :, :, DH:DH + 1], 1.0).then_inc(s_masked, 1)
            dve.memset(v_aug[1][:, :, :, DH:DH + 1], 1.0).then_inc(s_masked, 1)
            dve.memset(mn[:, :], 0.0).then_inc(pt_even, 1)
            dve.memset(rden[:, :], 0.0).then_inc(o_sb, 1)
            dve.memset(cc[:, :], 1.0)
            dve.memset(m16[:, :], 0.0).then_inc(c_ready, 1)
            dve.memset(sm[:, :], 0.0).then_inc(rd["y"], 1)
            dve.memset(dot2[:, :], 0.0).then_inc(acc_sb, 1)
            dve.memset(mv2[:, :, :], 0.0).then_inc(zT_lo_s, 1)

            def moments(b, p, bp):
                dve.wait_ge(batch_in[p], 32 * (bp + 1))
                for j in range(TT):
                    dve.bn_stats(st6[:, j, :], x_all[:, bass.ds(2 * b + j, 1), :].rearrange("p a d -> p (a d)"))
                    dve.bn_stats(st6[:, TT + j, :], c_in[p][:, j, :]).then_inc(small_v, 1)
                dve.wait_ge(small_v, 2 * b + 2)
                dve.sem_inc(turn_v)
                for j in range(4):
                    last = dve.bn_aggr(mv[:, j, :], st6[:, j, :])
                last.then_inc(mv_ready, 1)

            def normalise(b, p, first=False):
                dve.wait_ge(rstd_ready, b + 1)
                if not first:
                    dve.wait_ge(ps["cT"], b)
                for j in range(TT):
                    dve.tensor_scalar(ln[:, j, :], x_all[:, bass.ds(2 * b + j, 1), :].rearrange("p a d -> p (a d)"),
                                      mv[:, j, 0:1], rstd[:, j:j + 1], ALU.subtract, ALU.mult)
                    dve.tensor_scalar(cn[:, j, 0:DC], c_in[p][:, j, :],
                                      mv[:, TT + j, 0:1], rstd[:, TT + j:TT + j + 1], ALU.subtract, ALU.mult)
                    last = dve.tensor_scalar(cn[:, j, DC:DC + 64], c_in[p][:, j, P:DC],
                                             mv[:, TT + j, 0:1], rstd[:, TT + j:TT + j + 1], ALU.subtract, ALU.mult)
                last.then_inc(ln_ready, 1)

            def high_parts(f):
                dve.wait_ge(rd["lnT"], f + 1)
                dve.tensor_copy(lnT_hi[:, :, :], lnT[:, :, :]).then_inc(lnT_hi_ready, 1)
                dve.wait_ge(rd["cT"], f + 1)
                dve.tensor_copy(cT_hi[:, :, :], cT[:, :, :]).then_inc(cT_hi_ready, 1)
                dve.wait_ge(cT_hi_ready, f + 1)
                dve.tensor_tensor(cT_hi[DH:P, 1, :], cT[DH:P, 1, :], cT_hi[DH:P, 1, :].bitcast(F32), ALU.subtract
                                  ).then_inc(cT_stacked, 1)

            def latent_values(f, fp):
                dve.wait_ge(ps["v01"], f + 1)
                dve.tensor_copy(v_aug[fp][:, 0:TT, :, 0:DH],
                                kind_bank["v01"][:, :].rearrange("p (j h d) -> p j h d", j=TT, h=HEADS)
                                ).then_inc(rd["v01"], 1)

            def square_sums_lat(f):
                dve.wait_ge(rd["qk1"], f + 1)
                dve.tensor_reduce(ss[:, 0:16], sq[:, 0:4, :].rearrange("p a (h d) -> p (a h) d", d=DH),
                                  AX_X, ALU.add).then_inc(ss_lat, 1)

            def scale_lat(f):
                dve.wait_ge(rr_lat, f + 1)
                v = qk[:, :, :].rearrange("p j (h d) -> p (j h) d", d=DH)
                dve.tensor_tensor(v, v, rr[:, 0:16].rearrange("p (h o) -> p h o", o=1).broadcast_to([P, 16, DH]),
                                  ALU.mult).then_inc(lat_scaled, 1)

            def square_sums_ctx(f):
                dve.wait_ge(rd["kv1"], f + 1)
                dve.tensor_reduce(ss[:, 16:24], sq[:, 4:6, :].rearrange("p a (h d) -> p (a h) d", d=DH),
                                  AX_X, ALU.add).then_inc(ss_ctx, 1)

            def mask_and_min(t, units, p):
                if 0 in units:
                    dve.wait_ge(mask_ready, t + 1)
                for u in units:
                    dve.wait_ge(s_ps, 8 * t + u + 1)
                    dve.sem_inc(turn_v)
                    dve.tensor_tensor_reduce(prob[:, u, :], s_bank[u % 2][:, :], maskb[p][:, :], 1.0, BIG,
                                             ALU.add, ALU.min, mn[:, u:u + 1]).then_inc(s_masked, 1)

            def probT_even(t, u):
                dve.wait_ge(pt_ps, 8 * t + u + 1)
                if u >= 4:
                    dve.wait_ge(pv_done, 8 * t + u - 3)
                dve.tensor_copy(probT[:, u % 4, :, :].rearrange("p k q -> p (k q)"), pt_bank[0][:, :]
                                ).then_inc(pt_even, 1)

            def normalise_out(t, qt):
                dve.wait_ge(pv_done, 8 * t + 4 * qt + 4)
                o = o_bank[:, 0:HEADS * (DH + 1)].rearrange("p (h d) -> p h d", d=DH + 1)
                dve.reciprocal(rden[:, :], o[:, :, DH:DH + 1].rearrange("p h o -> p (h o)")).then_inc(o_rcp, 1)
                dve.wait_ge(o_rcp, 2 * t + qt + 1)
                dve.tensor_tensor(o_n[:, qt, :].rearrange("p (h d) -> p h d", d=DH), o[:, :, 0:DH],
                                  rden[:, :].rearrange("p (h o) -> p h o", o=1).broadcast_to([P, HEADS, DH]),
                                  ALU.mult).then_inc(o_sb, 1)

            def qT_out(f):
                dve.wait_ge(ps["qT"], f + 1)
                dve.tensor_scalar(qT[:, :, :].rearrange("p c n -> p (c n)"), kind_bank["qT"][:, :],
                                  neg_gqk[:, 0:1], None, ALU.mult).then_inc(rd["qT"], 1)

            def residual(t):
                dve.wait_ge(ps["y"], t + 1)
                dve.wait_ge(xbo_ready, t + 1)
                xt = x_all[:, bass.ds(2 * t, TT), :].rearrange("p j d -> p (j d)")
                dve.tensor_tensor(x2[:, :, :].rearrange("p j d -> p (j d)"), kind_bank["y"][:, :], xt, ALU.add
                                  ).then_inc(rd["y"], 1)

            def residual_stats(t):
                dve.wait_ge(rd["y"], t + 2)
                for j in range(TT):
                    dve.bn_stats(st6b[:, j, :], x2[:, j, :])
                    last = dve.tensor_tensor_reduce(o_n[:, j, :], x2[:, j, :], row_b[:, 3, :], 1.0, 0.0,
                                                    ALU.mult, ALU.add, dot2[:, j:j + 1])
                last.then_inc(x2_read, 1)
                dve.wait_ge(x2_read, t + 1)
                dve.tensor_copy(dots[:, bass.ds(2 * t, TT)], dot2[:, :])
                dve.bn_aggr(mv2[:, 0, :], st6b[:, 0, :])
                dve.bn_aggr(mv2[:, 1, :], st6b[:, 1, :]).then_inc(mv2_ready, 1)
                dve.wait_ge(mv2_ready, t + 1)
                dve.tensor_copy(mean2[:, bass.ds(2 * t, TT)], mv2[:, :, 0:1].rearrange("p j o -> p (j o)")
                                ).then_inc(x2_stats, 1)

            def step(t, p, th, more=True):
                f, n = t + 1, t + 2
                mask_and_min(t, range(2, 6), p)
                square_sums_lat(f)
                mask_and_min(t, (6, 7), p)
                probT_even(t, 0)
                if more:
                    moments(n, p, th)
                square_sums_ctx(f)
                probT_even(t, 2)
                scale_lat(f)
                probT_even(t, 4)
                normalise_out(t, 0)
                if more:
                    normalise(n, p)
                probT_even(t, 6)
                latent_values(f, 1 - p)
                normalise_out(t, 1)
                qT_out(f)
                if more:
                    high_parts(n)
                residual(t)
                mask_and_min(f, (0, 1), 1 - p)
                if more:
                    residual_stats(t)

            moments(0, 0, 0)
            dve.wait_ge(vecs_in, 16)
            dve.tensor_tensor(neg_gqk[:, :], vk[:, 4:5], vk[:, 5:6], ALU.mult).then_inc(setup_v, 1)
            dve.wait_ge(setup_v, 1)
            dve.tensor_scalar(neg_gqk[:, :], neg_gqk[:, :], -float(DH) ** -0.5, None, ALU.mult).then_inc(setup_v, 1)
            normalise(0, 0, first=True)
            dve.wait_ge(wlat_hi_s, 1)
            dve.tensor_sub(wlat_lo[:, :, :], wlat_raw, wlat_hi[:, :, :].bitcast(F32)).then_inc(wlat_lo_s, 1)
            high_parts(0)
            dve.wait_ge(wctx_hi_s, 1)
            dve.tensor_sub(wctx_lo[:, :, :], wctx_raw, wctx_hi[:, :, :].bitcast(F32)).then_inc(wctx_lo_s, 1)
            moments(1, 1, 0)
            normalise(1, 1)
            square_sums_lat(0)
            latent_values(0, 0)
            square_sums_ctx(0)
            scale_lat(0)
            high_parts(1)
            dve.wait_ge(setup_v, 2)
            qT_out(0)
            dve.wait_ge(rows_in, 16)
            dve.tensor_reduce(rt_sum[:, :], row_b[:, 3, :], AX_X, ALU.add).then_inc(setup_v, 1)
            mask_and_min(0, (0, 1), 0)
            with dve.Fori(0, (B - 2) // 2) as i:
                step(2 * i, 0, i + 1)
                step(2 * i + 1, 1, i + 1)
            step(B - 2, 0, None, more=False)
            mask_and_min(B - 1, range(2, 8), 1)

            def z_tiles(g):
                for j in range(4):
                    last = dve.tensor_scalar(z[:, j, :], x_all[:, bass.ds(4 * g + j, 1), :].rearrange("p a d -> p (a d)"),
                                             mean2[:, bass.ds(4 * g + j, 1)], zs_col(g, j), ALU.subtract, ALU.mult)
                last.then_inc(z_ready, 1)

            def zs_col(g, j):
                return zr[:, bass.ds(2 * g + j // TT, 1), 1, j % TT:j % TT + 1].rearrange("p b o -> p (b o)")

            def zT_low(g, kts=(0, 1), first=False):
                for kt in kts:
                    dve.wait_ge(zT_hi_s, 2 * g + kt + 1)
                    src = bank[1 + kt] if first else bank[7]
                    dve.tensor_tensor(zT_lo[:, kt, :], src[:, :], zT_hi[:, kt, :].bitcast(F32), ALU.subtract
                                      ).then_inc(zT_lo_s, 1)

            def h_low(g, m):
                dve.wait_ge(h_hi_s, HT * g + m + 1)
                dve.tensor_tensor(h_lo[m % 3][:, :], h_raw[m % 3], h_hi[m % 3][:, :].bitcast(F32), ALU.subtract
                                  ).then_inc(h_lo_s, 1)

            def sums_out(g, heavy):
                dve.wait_ge(h_used, HT * (g + 1))
                dve.wait_ge(x_biased, g + 1)
                for j in range(4):
                    xt = x_all[:, bass.ds(4 * g + j, 1), :].rearrange("p a d -> p (a d)")
                    dve.tensor_tensor(xt, bank[j][:, 0:D], xt, ALU.add)
                    last = dve.tensor_tensor(heavy[:, j, :], bank[j][:, D:2 * D], row_b[:, 2, :], ALU.add)
                last.then_inc(acc_sb, 1)

            def final(g, heavy):
                dve.wait_ge(acc_sb, g + 2)
                for j in range(4):
                    xt = x_all[:, bass.ds(4 * g + j, 1), :].rearrange("p a d -> p (a d)")
                    last = dve.scalar_tensor_tensor(xt, heavy[:, j, :], sel[:, j % TT, bass.ds(2 * g + j // TT, 1)], xt,
                                                    ALU.mult, ALU.add)
                last.then_inc(fin, 1)

            def descent(lo, hi):
                for it in range(lo, hi):
                    dve.wait_ge(c_ready, it + 1)
                    dve.tensor_scalar(m16[:, :], e16[:, :], cc[:, 0:1], None, ALU.min, ALU.add, accum_out=cc[:, 2:3]
                                      ).then_inc(c_sum, 1)
                    dve.wait_ge(c_sum, it + 1)
                    dve.tensor_scalar(cc[:, 0:1], cc[:, 2:3], 1.0 / N, 1e-37, ALU.mult, ALU.max).then_inc(c_ready, 1)

            def multiplier():
                dve.wait_ge(c_ready, ITERS)
                dve.reciprocal(cc[:, 3:4], cc[:, 0:1]).then_inc(c_ready, 1)
                dve.wait_ge(c_ready, ITERS + 1)
                dve.tensor_scalar(m16[:, :], e16[:, :], cc[:, 3:4], 1.0, ALU.mult, ALU.min).then_inc(c_ready, 1)
                dve.wait_ge(c_ready, ITERS + 2)
                dve.tensor_scalar(s16[:, :], m16[:, :], -1.0, 1.0, ALU.mult, ALU.add).then_inc(c_ready, 1)
                dve.wait_ge(c_ready, ITERS + 3)
                dve.tensor_tensor(s16[:, :], s16[:, :], m16[:, :], ALU.add).then_inc(sel16_ready, 1)

            def score_tokens():
                dve.wait_ge(x2_stats, B)
                dve.tensor_scalar(sm[:, :], mean2[:, :], rt_sum[:, 0:1], None, ALU.mult).then_inc(descent_v, 1)
                dve.wait_ge(descent_v, 1)
                dve.tensor_tensor(sm[:, :], dots[:, :], sm[:, :], ALU.subtract).then_inc(descent_v, 1)
                dve.wait_ge(descent_v, 2)
                dve.wait_ge(zr_ready, B)
                dve.tensor_tensor(s_tok[:, :].rearrange("p (b j) -> p b j", j=TT),
                                  sm[:, :].rearrange("p (b j) -> p b j", j=TT),
                                  zr[:, :, 0, :], ALU.mult).then_inc(s_ready, 1)

            def score_exponents():
                dve.wait_ge(s16_ps, 1)
                dve.tensor_scalar(e16[:, :], bank[7][0:B, 0:N], 0.0, None, ALU.min).then_inc(s16_read, 1)
                dve.wait_ge(s16_read, 1)
                dve.tensor_reduce(cc[:, 1:2], e16[:, :], AX_X, ALU.max).then_inc(descent_v, 1)
                dve.wait_ge(descent_v, 3)
                dve.tensor_scalar(e16[:, :], e16[:, :], cc[:, 1:2], None, ALU.subtract).then_inc(e_ready, 1)

            SLOTS = {(g, m): i for i, (g, m) in enumerate([(0, m) for m in range(5, HT)]
                                                          + [(g, m) for g in (1, 2) for m in range(HT)])}

            def descend_in(g, m):
                i = SLOTS[g, m]
                descent((ITERS - 1) * i // len(SLOTS), (ITERS - 1) * (i + 1) // len(SLOTS))

            def selection_out():
                dve.wait_ge(sel_ps, 1)
                dve.tensor_copy(sel[:, :, :].rearrange("p j b -> p (j b)"), bank[7][:, 0:TT * B]).then_inc(sel_ready, 1)
                dve.wait_ge(sel_ready, 1)

            def ffn(g, heavy, more=True, descend=False, select=False, finish=()):
                for m in range(HT):
                    h_low(g, m)
                    if m == 2 and more:
                        z_tiles(g + 1)
                    if select and m == 2:
                        selection_out()
                    if 3 <= m < 3 + len(finish):
                        final(*finish[m - 3])
                    if more and m == HT - 1:
                        zT_low(g + 1, (0,))
                    if descend:
                        descend_in(g, m)
                if more:
                    zT_low(g + 1, (1,))
                sums_out(g, heavy)

            probT_even(B - 1, 0)
            dve.wait_ge(x2_kept, TT)
            dve.wait_ge(zr_ready, TT)
            z_tiles(0)
            probT_even(B - 1, 2)
            residual_stats(B - 2)
            probT_even(B - 1, 4)
            normalise_out(B - 1, 0)
            probT_even(B - 1, 6)
            zT_low(0, first=True)
            normalise_out(B - 1, 1)
            h_low(0, 0)
            h_low(0, 1)
            dve.wait_ge(zr_ready, B - 1)
            residual(B - 1)
            residual_stats(B - 1)
            h_low(0, 2)
            score_tokens()
            dve.wait_ge(x2_kept, B)
            z_tiles(1)
            h_low(0, 3)
            score_exponents()
            h_low(0, 4)
            dve.wait_ge(exp_ready, 1)
            for m in range(5, HT):
                h_low(0, m)
                if m == HT - 1:
                    zT_low(1, (0,))
                descend_in(0, m)
            zT_low(1, (1,))
            sums_out(0, hv[0])
            for g in (1, 2):
                ffn(g, hv[g], descend=True)
            multiplier()
            ffn(3, hv[2], select=True, finish=((0, hv[0]), (1, hv[1]), (2, hv[2])))
            with dve.Fori(4, PAIRS - 1) as g:
                ffn(g, hv[2], finish=((g - 1, hv[2]),))
            ffn(PAIRS - 1, hv[2], more=False, finish=((PAIRS - 2, hv[2]),))
            final(PAIRS - 1, hv[2])

        @block.scalar
        def _(act):
            act.dma_start(vecs_sb[:, :], vecs).then_inc(vecs_in, 16)
            act.dma_start(row_b[:, :, :], rows.rearrange("(o r) d -> o r d", o=1).broadcast_to([P, 4, D])
                          ).then_inc(rows_in, 16)

            def front_out(f, first=False):
                act.wait_ge(ps["lnT"], f + 1)
                if not first:
                    act.wait_ge(lnT_lo_ready, f)
                for k in range(2):
                    last = act.activation(lnT[:, k, :], kind_bank["lnT"][:, k * N:(k + 1) * N], ACT.Identity,
                                          bias=vk[:, 2 + k:3 + k], scale=vk[:, k:k + 1])
                last.then_inc(rd["lnT"], 1)
                act.wait_ge(ps["cT"], f + 1)
                if not first:
                    act.wait_ge(cT_lo_ready, f)
                    act.wait_ge(cT_stacked, f)
                for k in range(2):
                    last = act.activation(cT[:, k, :], kind_bank["cT"][:, k * N:(k + 1) * N], ACT.Identity,
                                          bias=vc[:, 2 + k:3 + k], scale=vc[:, k:k + 1])
                last.then_inc(rd["cT"], 1)

            def qk_out(f, j, first=False):
                act.wait_ge(ps[f"qk{j}"], f + 1)
                if j == 0 and not first:
                    act.wait_ge(ps["kT1"], f)
                    act.wait_ge(ss_ctx, f)
                act.copy(qk[:, j, :], kind_bank[f"qk{j}"][:, :])
                act.activation(sq[:, 2 * j:2 * j + 2, :].rearrange("p a d -> p (a d)"), kind_bank[f"qk{j}"][:, :],
                               ACT.Square).then_inc(rd[f"qk{j}"], 1)

            def kv_out(f, fp):
                for j in range(TT):
                    act.wait_ge(ps[f"kv{j}"], f + 1)
                    act.copy(kc[:, j, :], kind_bank[f"kv{j}"][:, 0:D])
                    act.activation(sq[:, 4 + j, :], kind_bank[f"kv{j}"][:, 0:D], ACT.Square)
                    act.copy(v_aug[fp][:, TT + j, :, 0:DH],
                             kind_bank[f"kv{j}"][:, D:2 * D].rearrange("p (h d) -> p h d", h=HEADS)
                             ).then_inc(rd[f"kv{j}"], 1)

            def kT_out(f, c):
                act.wait_ge(ps[f"kT{c}"], f + 1)
                act.copy(kT[:, c, :], kind_bank[f"kT{c}"][:, :]).then_inc(rd[f"kT{c}"], 1)

            def oT_out(t):
                act.wait_ge(ps["oT"], t + 1)
                act.copy(o_T[:, :, :].rearrange("p c n -> p (c n)"), kind_bank["oT"][:, :]).then_inc(rd["oT"], 1)

            def keep_x2(t):
                act.wait_ge(rd["y"], t + 2)
                act.copy(x_all[:, bass.ds(2 * t, TT), :], x2[:, :, :]).then_inc(x2_kept, 1)

            def exponentials(t, units):
                for u in units:
                    act.wait_ge(s_masked, 8 * t + u + 3)
                    act.activation(prob[:, u, :], prob[:, u, :], ACT.Exp, bias=mn[:, u:u + 1], scale=-1.0
                                   ).then_inc(p_ready, 1)

            def probT_odd(t, u):
                act.wait_ge(pt_ps, 8 * t + u + 1)
                if u >= 4:
                    act.wait_ge(pv_done, 8 * t + u - 3)
                act.copy(probT[:, u % 4, :, :].rearrange("p k q -> p (k q)"), pt_bank[1][:, :]).then_inc(pt_odd, 1)

            def prepare_weights(part):
                if part < 2:
                    if part == 0:
                        act.wait_ge(w1_in, 16)
                    for c, g in ((slice(0, HID_L), part), (slice(HID_L, HT * P), 2 + part)):
                        last = act.activation(w1_raw[:, part, c], w1_raw[:, part, c], ACT.Identity, scale=vh[:, g:g + 1])
                    last.then_inc(w1_scaled, 1)
                elif part < 4:
                    k = part - 2
                    act.wait_ge(w1_scaled, k + 1)
                    act.copy(w1_hi[:, k, :], w1_raw[:, k, :]).then_inc(w_hi_s, 1)
                else:
                    if part == 4:
                        act.wait_ge(w2_in, 16)
                    m = slice(HT * (part - 4) // 4, HT * (part - 3) // 4)
                    act.copy(w2_hi[:, m, :], w2_raw[:, m, :]).then_inc(w_hi_s, 1)

            act.wait_ge(vecs_in, 16)
            act.copy(cred[:, 0:1], vk[:, 0:1]).then_inc(pt_odd, 1)
            act.copy(cred[:, 1:2], vk[:, 0:1]).then_inc(rd["oT"], 1)
            act.copy(cred[:, 2:3], vk[:, 0:1]).then_inc(gelu_done, 3)
            act.wait_ge(wlat_in, 16)
            act.copy(wlat_hi[:, :, :], wlat_raw).then_inc(wlat_hi_s, 1)
            front_out(0, first=True)
            act.wait_ge(wctx_in, 16)
            act.copy(wctx_hi[:, :, :], wctx_raw).then_inc(wctx_hi_s, 1)
            for j in range(TT):
                qk_out(0, j, first=True)
            kv_out(0, 0)
            front_out(1)
            kT_out(0, 0)
            kT_out(0, 1)

            def step(t, p, more=True, weights=None):
                f, n = t + 1, t + 2
                exponentials(t, (0, 1))
                qk_out(f, 0)
                exponentials(t, (2, 3))
                qk_out(f, 1)
                exponentials(t, (4, 5, 6, 7))
                kv_out(f, 1 - p)
                for u in (1, 3, 5, 7):
                    if weights is not None:
                        prepare_weights(weights + u // 2)
                    probT_odd(t, u)
                if more:
                    front_out(n)
                kT_out(f, 0)
                oT_out(t)
                kT_out(f, 1)
                keep_x2(t)

            step(0, 0, weights=0)
            step(1, 1, weights=4)
            with act.Fori(1, (B - 2) // 2) as i:
                step(2 * i, 0)
                step(2 * i + 1, 1)
            step(B - 2, 0, more=False)
            exponentials(B - 1, range(8))

            def zT_high(g, first=False):
                for kt in range(2):
                    src = bank[1 + kt] if first else bank[7]
                    act.wait_ge(zT_ps, 2 * g + kt + 1)
                    act.copy(zT_hi[:, kt, :], src[:, :]).then_inc(zT_hi_s, 1)

            def gelu(g, m, early):
                act.wait_ge(h_ps, HT * g + m + 1)
                if not early:
                    act.wait_ge(h_lo_s, HT * g + m - 2)
                act.activation(h_raw[m % 3], bank[4 + m % 3][:, :], ACT.Gelu, bias=vh[:, 4 + m:5 + m]
                               ).then_inc(gelu_done, 1)
                act.wait_ge(gelu_done, HT * g + m + 4)
                if not early:
                    act.wait_ge(h_used, HT * g + m - 2)
                act.copy(h_hi[m % 3][:, :], h_raw[m % 3]).then_inc(h_hi_s, 1)

            def ffn(g, more=True):
                for m in range(HT):
                    gelu(g, m, False)
                if more:
                    zT_high(g + 1)

            probT_odd(B - 1, 1)
            probT_odd(B - 1, 3)
            zT_high(0, first=True)
            probT_odd(B - 1, 5)
            probT_odd(B - 1, 7)
            gelu(0, 0, True)
            oT_out(B - 1)
            gelu(0, 1, True)
            keep_x2(B - 1)
            for m in range(2, 6):
                gelu(0, m, m < 3)
            act.wait_ge(e_ready, 1)
            act.activation(e16[:, :], e16[:, :], ACT.Exp).then_inc(exp_ready, 1)
            for m in range(6, HT):
                gelu(0, m, False)
            zT_high(1)
            with act.Fori(1, PAIRS - 1) as g:
                ffn(g)
            ffn(PAIRS - 1, more=False)

        @block.gpsimd
        def _(pool):
            pool.memset(neg_half[:, :], -0.5).then_inc(setup_p, 1)
            pool.memset(maskb[0][:, :], 0.0).then_inc(setup_p, 1)
            pool.memset(maskb[1][:, :], 0.0).then_inc(setup_p, 1)
            pool.wait_ge(setup_p, 3)

            def inverse_std(b):
                pool.wait_ge(mv_ready, b + 1)
                pool.sem_inc(turn_p)
                v = mv[:, :, 1:2].rearrange("p t o -> p (t o)")
                pool.tensor_scalar(rstd[:, 0:TT], v[:, 0:TT], 1.0 + LN_EPS, LN_EPS * LN_EPS, ALU.mult, ALU.add)
                pool.tensor_scalar(rstd[:, TT:4], v[:, TT:4], 1.0, LN_EPS, ALU.mult, ALU.add).then_inc(pool_step, 1)
                pool.wait_ge(pool_step, b + 1)
                pool.tensor_tensor(rstd[:, :], rstd[:, :], neg_half[:, 0:4], ALU.pow).then_inc(rstd_ready, 1)

            def low_parts(f):
                pool.wait_ge(lnT_hi_ready, f + 1)
                pool.tensor_tensor(lnT_lo[:, :, :], lnT[:, :, :], lnT_hi[:, :, :].bitcast(F32), ALU.subtract
                                   ).then_inc(lnT_lo_ready, 1)
                pool.wait_ge(cT_hi_ready, f + 1)
                pool.tensor_tensor(cT_lo[:, :], cT[:, 0, :], cT_hi[:, 0, :].bitcast(F32), ALU.subtract
                                   ).then_inc(cT_lo_ready, 1)

            def mask_bias(b, p):
                pool.tensor_copy(maskb[p][:, N:KEYS], mask_all[:, bass.ds(b * N, N)]).then_inc(pool_step2, 1)
                pool.wait_ge(pool_step2, b + 1)
                pool.sem_inc(turn_p)
                pool.tensor_scalar(maskb[p][:, N:KEYS], maskb[p][:, N:KEYS], -1.0, -BIG, ALU.add, ALU.mult
                                   ).then_inc(mask_ready, 1)

            def add_bo(b):
                pool.wait_ge(ln_ready, b + 1)
                xt = x_all[:, bass.ds(2 * b, TT), :]
                pool.tensor_tensor(xt, xt, row_b[:, 0:1, :].broadcast_to([P, TT, D]), ALU.add).then_inc(xbo_ready, 1)

            def inverse_norms(f, lat):
                c = slice(0, 16) if lat else slice(16, 24)
                pool.wait_ge(ss_lat if lat else ss_ctx, f + 1)
                pool.sem_inc(turn_p)
                pool.tensor_scalar(ss[:, c], ss[:, c], 1.0 / DH, 1e-16, ALU.mult, ALU.max).then_inc(norm_step, 1)
                pool.wait_ge(norm_step, 2 * f + (1 if lat else 2))
                pool.tensor_tensor(rr[:, c], ss[:, c], neg_half[:, c], ALU.pow).then_inc(rr_lat if lat else rr_ctx, 1)

            def scale_ctx(f):
                pool.wait_ge(rr_ctx, f + 1)
                v = kc[:, :, :].rearrange("p j (h d) -> p (j h) d", d=DH)
                pool.tensor_tensor(v, v, rr[:, 16:24].rearrange("p (h o) -> p h o", o=1).broadcast_to([P, 8, DH]),
                                   ALU.mult).then_inc(ctx_scaled, 1)

            def second_scales(t):
                pool.wait_ge(mv2_ready, t + 1)
                pool.sem_inc(turn_p)
                v = mv2[:, :, 1:2].rearrange("p j o -> p (j o)")
                pool.tensor_scalar(vtmp[:, 0, :], v, 1.0, LN_EPS, ALU.mult, ALU.add)
                pool.tensor_scalar(vtmp[:, 1, :], v, 1.0, 1e-24 / D * LN_EPS, ALU.mult, ALU.max).then_inc(zr_step, 1)
                pool.wait_ge(zr_step, t + 1)
                pool.tensor_tensor(zr[:, bass.ds(t, 1), :, :].rearrange("p b k j -> p (b k j)"),
                                   vtmp[:, :, :].rearrange("p k j -> p (k j)"), neg_half[:, 0:4], ALU.pow
                                   ).then_inc(zr_ready, 1)

            inverse_std(0)
            low_parts(0)
            inverse_std(1)
            inverse_norms(0, True)
            inverse_norms(0, False)
            scale_ctx(0)
            pool.wait_ge(mask_in, 16)
            mask_bias(0, 0)
            low_parts(1)
            pool.wait_ge(rows_in, 16)
            add_bo(0)
            mask_bias(1, 1)
            add_bo(1)

            def w1_low():
                for k in range(2):
                    pool.wait_ge(w_hi_s, k + 1)
                    pool.tensor_tensor(w1_lo[:, k, :], w1_raw[:, k, :], w1_hi[:, k, :].bitcast(F32), ALU.subtract
                                       ).then_inc(w_lo_s, 1)

            def w2_low():
                for c in range(4):
                    pool.wait_ge(w_hi_s, c + 3)
                    m = slice(HT * c // 4, HT * (c + 1) // 4)
                    pool.tensor_tensor(w2_lo[:, m, :], w2_raw[:, m, :], w2_hi[:, m, :].bitcast(F32), ALU.subtract
                                       ).then_inc(w_lo_s, 1)

            def step(t, p, more=True, weights=None):
                f, n = t + 1, t + 2
                inverse_norms(f, True)
                if more:
                    inverse_std(n)
                inverse_norms(f, False)
                scale_ctx(f)
                if weights is not None:
                    weights()
                if more:
                    low_parts(n)
                    mask_bias(n, p)
                    add_bo(n)
                second_scales(t)

            step(0, 0, weights=w1_low)
            step(1, 1, weights=w2_low)
            with pool.Fori(1, (B - 2) // 2) as i:
                step(2 * i, 0)
                step(2 * i + 1, 1)
            step(B - 2, 0, more=False)
            second_scales(B - 1)

            def bias_x(g):
                pool.wait_ge(z_ready, g + 1)
                xt = x_all[:, bass.ds(4 * g, 4), :]
                pool.tensor_tensor(xt, xt, row_b[:, 1:2, :].broadcast_to([P, 4, D]), ALU.add).then_inc(x_biased, 1)

            with pool.Fori(0, PAIRS) as g:
                bias_x(g)


def kernel(**inputs):
    import concourse.bacc as bacc
    from concourse.bass_utils import run_bass_kernel_spmd

    def get(name):
        return np.asarray(inputs[name])

    def cols(v):
        return np.ascontiguousarray(v.reshape(-1, P).T)

    def pre(name):
        return get("L0_ffn_" + name)

    w_lat = np.concatenate([get("L0_xattn_Wq").T, get("L0_xattn_Wlkv").T], axis=1)
    w_ctx = get("L0_xattn_Wkv").T
    w_ctx = np.concatenate([w_ctx, w_ctx[P:DC]], axis=0)

    def ctx_vec(v):
        return cols(np.concatenate([v, v[P:DC]]))

    def head_vec(v):
        return np.concatenate([v, v])[:, None]

    arrays = {
        "x": get("x"),
        "ctx_in": get("ctx_768"),
        "mask": get("mask_BxS2_bk0"),
        "w_lat": w_lat,
        "w_ctx": w_ctx,
        "w_o": get("L0_xattn_Wo").T,
        "w1": np.concatenate([pre("light_w1"), pre("heavy_w1")], axis=1),
        "w2": np.concatenate([pre("light_w2"), pre("heavy_w2")], axis=0),
        "vecs": np.concatenate([
            cols(get("L0_xattn_ln_l_g")), cols(get("L0_xattn_ln_l_b")),
            head_vec(get("L0_xattn_qn_g")), head_vec(get("L0_xattn_kn_g")),
            ctx_vec(get("L0_xattn_ln_x_g")), ctx_vec(get("L0_xattn_ln_x_b")),
            cols(pre("light_gamma")), cols(pre("heavy_gamma")), cols(pre("light_b1")), cols(pre("heavy_b1")),
            np.eye(P, dtype=np.float32)], axis=1),
        "rows": np.stack([get("L0_xattn_bo"), pre("light_b2"), pre("heavy_b2"), pre("routing_token")]),
    }
    arrays = {k: np.ascontiguousarray(v) for k, v in arrays.items()}
    nc = bacc.Bacc("TRN2", target_bir_lowering=False, num_devices=1)
    aps = [nc.dram_tensor("in_" + k, v.shape, mybir.dt.from_np(v.dtype), kind="ExternalInput").ap()
           for k, v in arrays.items()]
    out = nc.dram_tensor("out_0", (B, N, D), F32, kind="ExternalOutput").ap()
    build(nc, *aps, out)
    r = run_bass_kernel_spmd(nc, [{"in_" + k: v for k, v in arrays.items()}], core_ids=[0])
    return r.results[0]["out_0"]
```

```python
from contextlib import ExitStack

import numpy as np

import concourse.bass as bass
from concourse import mybir

ALU = mybir.AluOpType
ACT = mybir.ActivationFunctionType
F32 = mybir.dt.float32
F32R = mybir.dt.float32r
U8 = mybir.dt.uint8
AX_X = mybir.AxisListType.X

P = 128
B = 16
N = 256
D = 256
DC = 192
HEADS = 4
DH = 64
KEYS = 2 * N
TT = N // P
KT = KEYS // P
TILES = B * TT
PAIRS = B // 2
HID_L = 128
HID_H = 1024
HT = (HID_L + HID_H) // P
ITERS = 50
LN_EPS = 1e-5
BIG = 3.0e38


def build(nc, x, ctx_in, mask, w_lat, w_ctx, w_o, w1, w2, vecs, rows, out):
    ctx = ExitStack()
    with ctx:
        def sb(name, shape, dt=F32):
            return ctx.enter_context(nc.sbuf_tensor(name, shape, dt))

        def sem(name):
            return ctx.enter_context(nc.semaphore(name))

        bank = [ctx.enter_context(nc.psum_tensor(f"bank{i}", [P, 512], F32)) for i in range(8)]

        x_all = sb("x_all", [P, TILES, D])
        wlat_hi = sb("wlat_hi", [P, 2, 3 * D], F32R)
        wlat_lo = sb("wlat_lo", [P, 2, 3 * D], F32R)
        wctx_hi = sb("wctx_hi", [P, 2, 2 * D], F32R)
        wctx_lo = sb("wctx_lo", [P, 2, 2 * D], F32R)
        wo_hi = sb("wo_hi", [P, 2, D], F32R)
        wo_lo = sb("wo_lo", [P, 2, D], F32R)
        w1_hi = sb("w1_hi", [P, 2, HT * P], F32R)
        w1_lo = sb("w1_lo", [P, 2, HT * P], F32R)
        w2_hi = sb("w2_hi", [P, HT, D], F32R)
        w2_lo = sb("w2_lo", [P, HT, D], F32R)
        vecs_sb = sb("vecs_sb", [P, 14 + HT + P])
        row_b = sb("row_b", [P, 4, D])
        neg_half = sb("neg_half", [P, 32])
        neg_gqk = sb("neg_gqk", [P, 1])
        rt_sum = sb("rt_sum", [P, 1])
        mean2 = sb("mean2", [P, TILES])
        zr = sb("zr", [P, B, 2, TT])
        x2 = sb("x2", [P, TT, D])
        st6b = sb("st6b", [P, TT, 6])
        mv2 = sb("mv2", [P, TT, 2])
        dot2 = sb("dot2", [P, TT])
        dot_terms = sb("dot_terms", [P, TT, D])
        dots = sb("dots", [P, TILES])
        mask_all = sb("mask_all", [P, B * N], U8)

        c_in = [sb(f"c_in{p}", [P, TT, DC]) for p in range(2)]
        st6 = sb("st6", [P, 4, 6])
        mv = sb("mv", [P, 4, 2])
        rstd = sb("rstd", [P, 4])
        ln = sb("ln", [P, TT, D])
        cn = sb("cn", [P, TT, DC + 64])
        lnT = sb("lnT", [P, 2, N])
        lnT_hi = sb("lnT_hi", [P, 2, N], F32R)
        lnT_lo = sb("lnT_lo", [P, 2, N], F32R)
        cT = sb("cT", [P, 2, N])
        cT_hi = sb("cT_hi", [P, 2, N], F32R)
        cT_lo = sb("cT_lo", [P, N], F32R)
        qk = sb("qk", [P, TT, 2 * D])
        kc = sb("kc", [P, TT, D])
        sq = sb("sq", [P, 6, D])
        ss = sb("ss", [P, 6 * HEADS])
        rr = sb("rr", [P, 6 * HEADS])
        v_aug = [sb(f"v_aug{p}", [P, KT, HEADS, DH + 1]) for p in range(2)]
        maskb = [sb(f"maskb{p}", [P, KEYS]) for p in range(2)]
        prob = sb("prob", [P, TT * HEADS, KEYS])
        mn = sb("mn", [P, TT * HEADS])
        probT = sb("probT", [P, 4, KT, P])
        rden = sb("rden", [P, HEADS])
        vtmp = sb("vtmp", [P, 2, TT])
        o_n = sb("o_n", [P, TT, D])
        oT_hi = sb("oT_hi", [P, 2, N], F32R)
        oT_lo = sb("oT_lo", [P, 2, N], F32R)

        z = qk[:, :, :].rearrange("p a b -> p (a b)").rearrange("p (j d) -> p j d", j=4)
        zT_hi = sb("zT_hi", [P, 2, 512], F32R)
        zT_lo = sb("zT_lo", [P, 2, 512], F32R)
        h_raw = [prob[:, 2 + i, :] for i in range(3)]
        h_hi = [sb(f"h_hi{i}", [P, 512], F32R) for i in range(3)]
        h_lo = [sb(f"h_lo{i}", [P, 512], F32R) for i in range(3)]
        qT_hi = h_hi[0][:, :].rearrange("p (c n) -> p c n", c=2)
        qT_lo = h_lo[0][:, :].rearrange("p (c n) -> p c n", c=2)
        kT_hi, kT_lo = zT_hi, zT_lo
        probT_flat = probT[:, :, :, :].rearrange("p a b c -> p (a b c)")
        hv = [probT_flat[:, i * 4 * D:(i + 1) * 4 * D].rearrange("p (a d) -> p a d", a=4) for i in range(2)]
        hv.append(sq[:, 0:4, :])
        sm = sb("sm", [P, TILES])
        s_tok = sb("s_tok", [P, TILES])
        cred = sb("cred", [P, 2])
        credit_v = sb("credit_v", [P, 1])
        s16 = sb("s16", [B, N])
        e16 = sb("e16", [B, N])
        m16 = sb("m16", [B, N])
        cc = sb("cc", [B, 4])
        sel = sb("sel", [P, TT, B])

        vk = vecs_sb[:, 0:6]
        vc = vecs_sb[:, 6:10]
        vh = vecs_sb[:, 10:14 + HT]
        ident = vecs_sb[:, 14 + HT:14 + HT + P]

        wctx_raw = prob[:, 5:7, :].rearrange("p a b -> p (a b)").rearrange("p (k n) -> p k n", k=2)
        wlat_raw = sq[:, :, :].rearrange("p a b -> p (a b)").rearrange("p (k n) -> p k n", k=2)
        wo_raw = prob[:, 7, :].rearrange("p (k n) -> p k n", k=2)
        w1_raw = x_all[:, TILES - 2 * HT:TILES - HT, :].rearrange("p a b -> p (a b)").rearrange("p (k n) -> p k n", k=2)
        w2_raw = x_all[:, TILES - HT:TILES, :]

        vecs_in, rows_in = sem("vecs_in"), sem("rows_in")
        wlat_in, wctx_in, w1_in, w2_in, wo_in, mask_in = (sem(s) for s in (
            "wlat_in", "wctx_in", "w1_in", "w2_in", "wo_in", "mask_in"))
        batch_in = [sem(f"batch_in{p}") for p in range(2)]
        out_done = sem("out_done")
        setup_v, setup_p = sem("setup_v"), sem("setup_p")
        wlat_hi_s, wctx_hi_s, wlat_lo_s, wctx_lo_s, wo_hi_s, wo_lo_s = (sem(s) for s in (
            "wlat_hi_s", "wctx_hi_s", "wlat_lo_s", "wctx_lo_s", "wo_hi_s", "wo_lo_s"))
        w1_scaled, w_hi_s, w_lo_s = sem("w1_scaled"), sem("w_hi_s"), sem("w_lo_s")
        kinds = ("qk0", "qk1", "v01", "kv0", "kv1", "lnT", "cT", "qT", "kT0", "oT", "kT1", "y")
        ps = {k: sem(k + "_ps") for k in kinds}
        rd = {k: sem(k + "_sb") for k in kinds}
        hi_s = {k: sem(k + "_hi_s") for k in ("qT", "kT0", "kT1", "oT")}
        mv_ready, rstd_ready, ln_ready, small_v = sem("mv_ready"), sem("rstd_ready"), sem("ln_ready"), sem("small_v")
        pool_step, pool_step2 = sem("pool_step"), sem("pool_step2")
        lnT_hi_ready, lnT_lo_ready = sem("lnT_hi_ready"), sem("lnT_lo_ready")
        cT_hi_ready, cT_stacked, cT_lo_ready = sem("cT_hi_ready"), sem("cT_stacked"), sem("cT_lo_ready")
        ss_lat, ss_ctx, rr_lat, rr_ctx = sem("ss_lat"), sem("ss_ctx"), sem("rr_lat"), sem("rr_ctx")
        lat_scaled, ctx_scaled = sem("lat_scaled"), sem("ctx_scaled")
        mask_ready, xbo_ready = sem("mask_ready"), sem("xbo_ready")
        s_ps, s_masked, p_ready = sem("s_ps"), sem("s_masked"), sem("p_ready")
        pt_ps = sem("pt_ps")
        pt_even, pt_odd = sem("pt_even"), sem("pt_odd")
        pv_done, o_rcp, o_sb = sem("pv_done"), sem("o_rcp"), sem("o_sb")
        x2_read, mv2_ready, x2_stats, x2_kept, zr_ready, zr_step = (sem(k) for k in (
            "x2_read", "mv2_ready", "x2_stats", "x2_kept", "zr_ready", "zr_step"))
        s_ready, s16_ps, s16_read, e_ready, exp_ready, sel16_ready, sel_ps, sel_ready = (sem(s) for s in (
            "s_ready", "s16_ps", "s16_read", "e_ready", "exp_ready", "sel16_ready", "sel_ps", "sel_ready"))
        descent_v, c_sum, c_ready = sem("descent_v"), sem("c_sum"), sem("c_ready")
        turn_v, turn_p = sem("turn_v"), sem("turn_p")
        x_biased, norm_step = sem("x_biased"), sem("norm_step")
        z_ready, zT_ps, zT_hi_s, zT_lo_s = sem("z_ready"), sem("zT_ps"), sem("zT_hi_s"), sem("zT_lo_s")
        h_ps, gelu_done, h_hi_s, h_lo_s, h_used, acc_sb, fin, last_s = (sem(s) for s in (
            "h_ps", "gelu_done", "h_hi_s", "h_lo_s", "h_used", "acc_sb", "fin", "last_s"))

        kind_bank = {k: bank[i % 3] for i, k in enumerate(kinds)}
        s_bank = [bank[3], bank[4]]
        pt_bank = [bank[5], bank[6]]
        kind_bank["oT"], kind_bank["y"] = pt_bank
        o_bank = bank[7]

        x_t = x.rearrange("b (j p) d -> p (b j) d", p=P)
        out_t = out.rearrange("b (j p) d -> p (b j) d", p=P)
        c_t = ctx_in.rearrange("b (j p) d -> p (b j) d", p=P)

        block = ctx.enter_context(nc.Block())

        @block.sync
        def _(sp):
            def load(b, p):
                sp.dma_start(x_all[:, bass.ds(2 * b, TT), :], x_t[:, bass.ds(2 * b, TT), :]).then_inc(batch_in[p], 16)
                sp.dma_start(c_in[p][:, :, :], c_t[:, bass.ds(2 * b, TT), :]).then_inc(batch_in[p], 16)

            load(0, 0)
            sp.dma_start(wlat_raw, w_lat.rearrange("(k p) n -> p k n", p=P)).then_inc(wlat_in, 16)
            sp.dma_start(wctx_raw, w_ctx.rearrange("(k p) n -> p k n", p=P)).then_inc(wctx_in, 16)
            load(1, 1)
            sp.dma_start(mask_all[:, :], mask.rearrange("(o b) n -> o (b n)", o=1).broadcast_to([P, B * N])).then_inc(mask_in, 16)
            sp.dma_start(wo_raw, w_o.rearrange("(k p) n -> p k n", p=P)).then_inc(wo_in, 16)
            sp.dma_start(w1_raw, w1.rearrange("(k p) n -> p k n", p=P)).then_inc(w1_in, 16)
            sp.dma_start(w2_raw, w2.rearrange("(k p) n -> p k n", p=P)).then_inc(w2_in, 16)
            def load_pairs(lo, hi):
                with sp.Fori(lo, hi) as i:
                    for p in range(2):
                        sp.wait_ge(ln_ready, 2 * i + p - 1)
                        load(2 * i + p, p)

            weights_from = (TILES - 2 * HT) // TT
            load_pairs(1, weights_from // 2)
            sp.wait_ge(w_lo_s, 6)
            load_pairs(weights_from // 2, B // 2)
            with sp.Fori(0, PAIRS - 1) as g:
                sp.wait_ge(fin, g + 1)
                sp.dma_start(out_t[:, bass.ds(4 * g, 4), :], x_all[:, bass.ds(4 * g, 4), :]).then_inc(out_done, 16)
            for i in range(2):
                sp.wait_ge(fin, PAIRS + i)
                t = slice(TILES - 4 + TT * i, TILES - 4 + TT * (i + 1))
                sp.dma_start(out_t[:, t, :], x_all[:, t, :]).then_inc(out_done, 16)
            sp.wait_ge(out_done, 16 * (PAIRS + 1))

        @block.tensor
        def _(pe):
            def take(kind, need):
                if need is not None:
                    pe.wait_ge(rd[need[0]], need[1])

            def split_products(dst, pairs):
                for n, (shi, slo, mhi, mlo) in enumerate(pairs):
                    for m, (s, v) in enumerate(((shi, mhi), (shi, mlo), (slo, mhi))):
                        last = pe.matmul(dst, s, v, start=(n == 0 and m == 0),
                                         stop=(n == len(pairs) - 1 and m == 2))
                return last

            def front_transposes(f, need_ln, need_c):
                pe.wait_ge(ln_ready, f + 1)
                take("lnT", need_ln)
                for kt in range(2):
                    for j in range(TT):
                        last = pe.transpose(kind_bank["lnT"][:, kt * N + j * P:kt * N + (j + 1) * P],
                                            ln[:, j, kt * P:(kt + 1) * P], ident[:, :])
                last.then_inc(ps["lnT"], 1)
                take("cT", need_c)
                for kt in range(2):
                    for j in range(TT):
                        last = pe.transpose(kind_bank["cT"][:, kt * N + j * P:kt * N + (j + 1) * P],
                                            cn[:, j, kt * P:(kt + 1) * P], ident[:, :])
                last.then_inc(ps["cT"], 1)

            def lat_pairs(j, c0, c1):
                t = slice(j * P, (j + 1) * P)
                return [(lnT_hi[:, kt, t], lnT_lo[:, kt, t], wlat_hi[:, kt, c0:c1], wlat_lo[:, kt, c0:c1])
                        for kt in range(2)]

            def project_qk(f, j, need):
                pe.wait_ge(lnT_hi_ready, f + 1)
                pe.wait_ge(lnT_lo_ready, f + 1)
                take(f"qk{j}", need)
                split_products(kind_bank[f"qk{j}"][:, :], lat_pairs(j, 0, 2 * D)).then_inc(ps[f"qk{j}"], 1)

            def project_v(f, need):
                take("v01", need)
                for j in range(TT):
                    last = split_products(kind_bank["v01"][:, j * D:(j + 1) * D], lat_pairs(j, 2 * D, 3 * D))
                last.then_inc(ps["v01"], 1)

            def project_ctx(f, js=range(TT)):
                pe.wait_ge(cT_stacked, f + 1)
                pe.wait_ge(cT_lo_ready, f + 1)
                for j in js:
                    take(f"kv{j}", (f"qk{j}", f + 1))
                    t = slice(j * P, (j + 1) * P)
                    dst = kind_bank[f"kv{j}"][:, :]
                    pe.matmul(dst, cT_hi[:, 1, t], wctx_hi[:, 1, :], start=True, stop=False)
                    pe.matmul(dst, cT_hi[0:DH, 1, t], wctx_lo[0:DH, 1, :], start=False, stop=False)
                    pe.matmul(dst, cT_hi[:, 0, t], wctx_hi[:, 0, :], start=False, stop=False)
                    pe.matmul(dst, cT_hi[:, 0, t], wctx_lo[:, 0, :], start=False, stop=False)
                    pe.matmul(dst, cT_lo[:, t], wctx_hi[:, 0, :], start=False, stop=True).then_inc(ps[f"kv{j}"], 1)

            def q_transposes(f):
                pe.wait_ge(lat_scaled, f + 1)
                take("qT", ("kv1", f + 1))
                for c in range(2):
                    for j in range(TT):
                        last = pe.transpose(kind_bank["qT"][:, c * N + j * P:c * N + (j + 1) * P],
                                            qk[:, j, c * P:(c + 1) * P], ident[:, :])
                last.then_inc(ps["qT"], 1)

            def k_transposes(f, c, need):
                if c == 0:
                    pe.wait_ge(ctx_scaled, f + 1)
                take(f"kT{c}", need)
                for t in range(KT):
                    src = qk[:, t, D + c * P:D + (c + 1) * P] if t < TT else kc[:, t - TT, c * P:(c + 1) * P]
                    last = pe.transpose(kind_bank[f"kT{c}"][:, t * P:(t + 1) * P], src, ident[:, :])
                last.then_inc(ps[f"kT{c}"], 1)

            def scores(t, u0):
                for k in {0: ("qT", "kT0"), 2: ("kT1",)}.get(u0, ()):
                    pe.wait_ge(rd[k], t + 1)
                for u in (u0, u0 + 1):
                    qt, h = divmod(u, HEADS)
                    pe.wait_ge(s_masked, 8 * t + u + 1)
                    r = slice(DH * (h % 2), DH * (h % 2) + DH)
                    q = slice(qt * P, (qt + 1) * P)
                    split_products(s_bank[h % 2][:, :], [(qT_hi[r, h // 2, q], qT_lo[r, h // 2, q],
                                                          kT_hi[r, h // 2, :], kT_lo[r, h // 2, :])]).then_inc(s_ps, 1)

            def prob_transposes(t, u):
                pe.wait_ge(p_ready, 8 * t + u + 1)
                if u == 1:
                    pe.wait_ge(rd["y"], t + 1)
                pe.wait_ge(pt_even if u % 2 == 0 else pt_odd, 4 * t + u // 2 + 1)
                for k in range(KT):
                    last = pe.transpose(pt_bank[u % 2][:, k * P:(k + 1) * P], prob[:, u, k * P:(k + 1) * P], ident[:, :])
                last.then_inc(pt_ps, 1)

            def weighted_values(t, u, p):
                qt, h = divmod(u, HEADS)
                pe.wait_ge(pt_even if u % 2 == 0 else pt_odd, 4 * t + u // 2 + 2)
                if u == 0:
                    pe.wait_ge(rd["v01"], t + 1)
                    pe.wait_ge(rd["kv1"], t + 1)
                if h == 0:
                    pe.wait_ge(o_sb, 2 * t + qt + 1)
                for k in range(KT):
                    last = pe.matmul(o_bank[:, h * (DH + 1):(h + 1) * (DH + 1)], probT[:, u % 4, k, :],
                                     v_aug[p][:, k, h, :], start=(k == 0), stop=(k == KT - 1))
                last.then_inc(pv_done, 1)

            def attend(t, p, units):
                for u in units:
                    if u < 8:
                        prob_transposes(t, u)
                    weighted_values(t, u - 1, p)

            def o_transposes(t, dst):
                pe.wait_ge(o_sb, 2 * t + 3)
                for c in range(2):
                    for j in range(TT):
                        last = pe.transpose(dst[:, c * N + j * P:c * N + (j + 1) * P],
                                            o_n[:, j, c * P:(c + 1) * P], ident[:, :])
                last.then_inc(ps["oT"], 1)

            def out_projection(t, dst):
                pe.wait_ge(rd["oT"], t + 2)
                for j in range(TT):
                    q = slice(j * P, (j + 1) * P)
                    last = split_products(dst[:, j * D:(j + 1) * D],
                                          [(oT_hi[:, c, q], oT_lo[:, c, q], wo_hi[:, c, :], wo_lo[:, c, :])
                                           for c in range(2)])
                last.then_inc(ps["y"], 1)

            pe.wait_ge(vecs_in, 16)
            front_transposes(0, None, None)
            pe.wait_ge(wlat_lo_s, 1)
            project_qk(0, 0, ("cT", 1))
            project_qk(0, 1, None)
            project_v(0, ("lnT", 1))
            pe.wait_ge(wctx_lo_s, 1)
            project_ctx(0)
            front_transposes(1, ("v01", 1), ("kv0", 1))
            q_transposes(0)
            k_transposes(0, 0, ("lnT", 2))
            k_transposes(0, 1, ("qT", 1))
            project_qk(1, 0, ("cT", 2))
            pe.wait_ge(wo_lo_s, 1)

            def step(t, p, more=True):
                f, n = t + 1, t + 2
                scores(t, 0)
                project_qk(f, 1, ("kT1", t + 1))
                scores(t, 2)
                prob_transposes(t, 0)
                scores(t, 4)
                project_ctx(f, (0,))
                scores(t, 6)
                prob_transposes(t, 1)
                project_ctx(f, (1,))
                weighted_values(t, 0, p)
                attend(t, p, range(2, 5))
                prob_transposes(t, 5)
                project_v(f, ("kT0", t + 1))
                weighted_values(t, 4, p)
                attend(t, p, (6,))
                prob_transposes(t, 7)
                if more:
                    front_transposes(n, ("v01", f + 1), ("kv0", f + 1))
                weighted_values(t, 6, p)
                weighted_values(t, 7, p)
                q_transposes(f)
                k_transposes(f, 0, ("lnT", n + 1) if more else ("v01", f + 1))
                o_transposes(t, kind_bank["oT"])
                if more:
                    project_qk(n, 0, ("cT", n + 1))
                k_transposes(f, 1, ("qT", f + 1))
                out_projection(t, kind_bank["y"])

            with pe.Fori(0, (B - 2) // 2) as i:
                step(2 * i, 0)
                step(2 * i + 1, 1)
            step(B - 2, 0, more=False)
            scores(B - 1, 0)
            scores(B - 1, 2)
            prob_transposes(B - 1, 0)
            scores(B - 1, 4)
            prob_transposes(B - 1, 1)
            scores(B - 1, 6)

            acc = bank[0:4]
            h_bank = bank[4:7]

            def z_transposes(g, kt, first=False):
                pe.wait_ge(z_ready, g + 1)
                if not first:
                    pe.wait_ge(zT_lo_s, 2 * g + kt + 1)
                dst = bank[1 + kt] if first else bank[7]
                for j in range(4):
                    last = pe.transpose(dst[:, j * P:(j + 1) * P], z[:, j, kt * P:(kt + 1) * P], ident[:, :])
                last.then_inc(zT_ps, 1)

            def hidden(g, m):
                pe.wait_ge(gelu_done, HT * g + m + 1)
                t = slice(m * P, (m + 1) * P)
                for k in range(2):
                    if m == 0:
                        pe.wait_ge(zT_hi_s, 2 * g + k + 1)
                        pe.wait_ge(zT_lo_s, 2 * g + k + 2)
                    for n, (w, v) in enumerate(((w1_hi, zT_hi), (w1_hi, zT_lo), (w1_lo, zT_hi))):
                        last = pe.matmul(h_bank[m % 3][:, :], w[:, k, t], v[:, k, :],
                                         start=(k == 0 and n == 0), stop=(k == 1 and n == 2))
                last.then_inc(h_ps, 1)

            def outputs(g, m, each=False):
                pe.wait_ge(h_hi_s, HT * g + m + 1)
                pe.wait_ge(h_lo_s, HT * g + m + 1)
                if m == 0:
                    pe.wait_ge(acc_sb, g + 1)
                c = slice(0, D) if m == 0 else slice(D, 2 * D)
                for j in range(4):
                    t = slice(j * P, (j + 1) * P)
                    terms = ((h_hi[m % 3][:, t], w2_hi[:, m, :]), (h_hi[m % 3][:, t], w2_lo[:, m, :]),
                             (h_lo[m % 3][:, t], w2_hi[:, m, :]))
                    for n, (s, v) in enumerate(terms):
                        last = pe.matmul(acc[j][:, c], s, v, start=(m <= 1 and n == 0),
                                         stop=(m in (0, HT - 1) and n == 2))
                    if each or j == 3:
                        last.then_inc(h_used, 1)

            def score_transposes():
                pe.wait_ge(s_ready, 1)
                for j in range(TT):
                    last = pe.transpose(bank[7][0:B, j * P:(j + 1) * P], s_tok[:, j:TILES:TT], ident[:, :])
                last.then_inc(s16_ps, 1)

            def selection_transposes():
                pe.wait_ge(sel16_ready, 1)
                for j in range(TT):
                    last = pe.transpose(bank[7][:, j * B:(j + 1) * B], s16[:, j * P:(j + 1) * P], ident[0:B, 0:B])
                last.then_inc(sel_ps, 1)

            def ffn(g, first=False, more=True, select=False):
                if not first:
                    hidden(g, 0)
                    hidden(g, 1)
                for m in range(HT):
                    if m + 2 < HT:
                        hidden(g, m + 2)
                    if first and m == 3:
                        score_transposes()
                    if first and m == 0:
                        pe.wait_ge(rd["y"], B + 1)
                    if select and m == 2:
                        selection_transposes()
                    if more and m == HT - 3:
                        if first:
                            pe.wait_ge(s16_read, 1)
                        if select:
                            pe.wait_ge(sel_ready, 1)
                        z_transposes(g + 1, 0)
                    if more and m == HT - 1:
                        z_transposes(g + 1, 1)
                    outputs(g, m, each=not more and m == HT - 1)

            weighted_values(B - 1, 0, 1)
            attend(B - 1, 1, range(2, 4))
            for kt in range(2):
                z_transposes(0, kt, first=True)
            attend(B - 1, 1, range(4, 9))
            pe.wait_ge(w_lo_s, 6)
            hidden(0, 0)
            o_transposes(B - 1, bank[0])
            hidden(0, 1)
            out_projection(B - 1, bank[2])
            ffn(0, first=True)
            with pe.Fori(1, 3) as g:
                ffn(g)
            ffn(3, select=True)
            with pe.Fori(4, PAIRS - 1) as g:
                ffn(g)
            ffn(PAIRS - 1, more=False)

        @block.vector
        def _(dve):
            dve.memset(v_aug[0][:, :, :, DH:DH + 1], 1.0).then_inc(s_masked, 1)
            dve.memset(v_aug[1][:, :, :, DH:DH + 1], 1.0).then_inc(s_masked, 1)
            dve.memset(mn[:, :], 0.0).then_inc(pt_even, 1)
            dve.memset(rden[:, :], 0.0).then_inc(o_sb, 1)
            dve.memset(credit_v[:, :], 0.0).then_inc(rd["oT"], 1)
            dve.memset(cc[:, :], 1.0)
            dve.memset(m16[:, :], 0.0).then_inc(c_ready, 1)
            dve.memset(sm[:, :], 0.0).then_inc(rd["y"], 1)
            dve.memset(dot2[:, :], 0.0).then_inc(acc_sb, 1)
            dve.memset(mv2[:, :, :], 0.0).then_inc(zT_lo_s, 1)

            def moments(b, p, bp):
                dve.wait_ge(batch_in[p], 32 * (bp + 1))
                for j in range(TT):
                    dve.bn_stats(st6[:, j, :], x_all[:, bass.ds(2 * b + j, 1), :].rearrange("p a d -> p (a d)"))
                    dve.bn_stats(st6[:, TT + j, :], c_in[p][:, j, :]).then_inc(small_v, 1)
                dve.wait_ge(small_v, 2 * b + 2)
                dve.sem_inc(turn_v)
                for j in range(4):
                    last = dve.bn_aggr(mv[:, j, :], st6[:, j, :])
                last.then_inc(mv_ready, 1)

            def normalise(b, p, first=False):
                dve.wait_ge(rstd_ready, b + 1)
                if not first:
                    dve.wait_ge(ps["cT"], b)
                for j in range(TT):
                    dve.tensor_scalar(ln[:, j, :], x_all[:, bass.ds(2 * b + j, 1), :].rearrange("p a d -> p (a d)"),
                                      mv[:, j, 0:1], rstd[:, j:j + 1], ALU.subtract, ALU.mult)
                    dve.tensor_scalar(cn[:, j, 0:DC], c_in[p][:, j, :],
                                      mv[:, TT + j, 0:1], rstd[:, TT + j:TT + j + 1], ALU.subtract, ALU.mult)
                    last = dve.tensor_scalar(cn[:, j, DC:DC + 64], c_in[p][:, j, P:DC],
                                             mv[:, TT + j, 0:1], rstd[:, TT + j:TT + j + 1], ALU.subtract, ALU.mult)
                last.then_inc(ln_ready, 1)

            def lat_high(f):
                dve.wait_ge(rd["lnT"], f + 1)
                dve.tensor_copy(lnT_hi[:, :, :], lnT[:, :, :]).then_inc(lnT_hi_ready, 1)

            def ctx_high(f):
                dve.wait_ge(rd["cT"], f + 1)
                dve.tensor_copy(cT_hi[:, :, :], cT[:, :, :]).then_inc(cT_hi_ready, 1)
                dve.wait_ge(cT_hi_ready, f + 1)
                dve.tensor_tensor(cT_hi[DH:P, 1, :], cT[DH:P, 1, :], cT_hi[DH:P, 1, :].bitcast(F32), ALU.subtract
                                  ).then_inc(cT_stacked, 1)

            def latent_values(f, fp):
                dve.wait_ge(ps["v01"], f + 1)
                dve.tensor_copy(v_aug[fp][:, 0:TT, :, 0:DH],
                                kind_bank["v01"][:, :].rearrange("p (j h d) -> p j h d", j=TT, h=HEADS)
                                ).then_inc(rd["v01"], 1)

            def square_sums_lat(f):
                dve.wait_ge(rd["qk1"], f + 1)
                dve.tensor_reduce(ss[:, 0:16], sq[:, 0:4, :].rearrange("p a (h d) -> p (a h) d", d=DH),
                                  AX_X, ALU.add).then_inc(ss_lat, 1)

            def scale_lat(f):
                dve.wait_ge(rr_lat, f + 1)
                v = qk[:, :, :].rearrange("p j (h d) -> p (j h) d", d=DH)
                dve.tensor_tensor(v, v, rr[:, 0:16].rearrange("p (h o) -> p h o", o=1).broadcast_to([P, 16, DH]),
                                  ALU.mult).then_inc(lat_scaled, 1)

            def square_sums_ctx(f):
                dve.wait_ge(rd["kv1"], f + 1)
                dve.tensor_reduce(ss[:, 16:24], sq[:, 4:6, :].rearrange("p a (h d) -> p (a h) d", d=DH),
                                  AX_X, ALU.add).then_inc(ss_ctx, 1)

            def mask_and_min(t, units, p):
                if 0 in units:
                    dve.wait_ge(mask_ready, t + 1)
                for u in units:
                    dve.wait_ge(s_ps, 8 * t + u + 1)
                    dve.sem_inc(turn_v)
                    dve.tensor_tensor_reduce(prob[:, u, :], s_bank[u % 2][:, :], maskb[p][:, :], 1.0, BIG,
                                             ALU.add, ALU.min, mn[:, u:u + 1]).then_inc(s_masked, 1)

            def probT_even(t, u):
                dve.wait_ge(pt_ps, 8 * t + u + 1)
                if u >= 4:
                    dve.wait_ge(pv_done, 8 * t + u - 3)
                dve.tensor_copy(probT[:, u % 4, :, :].rearrange("p k q -> p (k q)"), pt_bank[0][:, :]
                                ).then_inc(pt_even, 1)

            def normalise_out(t, qt):
                dve.wait_ge(pv_done, 8 * t + 4 * qt + 4)
                o = o_bank[:, 0:HEADS * (DH + 1)].rearrange("p (h d) -> p h d", d=DH + 1)
                dve.reciprocal(rden[:, :], o[:, :, DH:DH + 1].rearrange("p h o -> p (h o)")).then_inc(o_rcp, 1)
                dve.wait_ge(o_rcp, 2 * t + qt + 1)
                dve.tensor_tensor(o_n[:, qt, :].rearrange("p (h d) -> p h d", d=DH), o[:, :, 0:DH],
                                  rden[:, :].rearrange("p (h o) -> p h o", o=1).broadcast_to([P, HEADS, DH]),
                                  ALU.mult).then_inc(o_sb, 1)

            def qT_low(f):
                dve.wait_ge(hi_s["qT"], f + 1)
                dve.scalar_tensor_tensor(qT_lo.rearrange("p c n -> p (c n)"), kind_bank["qT"][:, :], neg_gqk[:, 0:1],
                                         qT_hi.rearrange("p c n -> p (c n)").bitcast(F32), ALU.mult, ALU.subtract
                                         ).then_inc(rd["qT"], 1)

            def kT_low(f, c):
                dve.wait_ge(hi_s[f"kT{c}"], f + 1)
                dve.tensor_tensor(kT_lo[:, c, :], kind_bank[f"kT{c}"][:, :], kT_hi[:, c, :].bitcast(F32), ALU.subtract
                                  ).then_inc(rd[f"kT{c}"], 1)

            def oT_low(t, src):
                dve.wait_ge(hi_s["oT"], t + 1)
                dve.tensor_tensor(oT_lo[:, :, :].rearrange("p c n -> p (c n)"), src[:, :],
                                  oT_hi[:, :, :].rearrange("p c n -> p (c n)").bitcast(F32), ALU.subtract
                                  ).then_inc(rd["oT"], 1)

            def residual(t, src):
                dve.wait_ge(ps["y"], t + 1)
                dve.wait_ge(xbo_ready, t + 1)
                xt = x_all[:, bass.ds(2 * t, TT), :].rearrange("p j d -> p (j d)")
                dve.tensor_tensor(x2[:, :, :].rearrange("p j d -> p (j d)"), src[:, :], xt, ALU.add
                                  ).then_inc(rd["y"], 1)

            def residual_terms(t, j):
                if j == 0:
                    dve.wait_ge(rd["y"], t + 2)
                dve.bn_stats(st6b[:, j, :], x2[:, j, :])
                last = dve.tensor_tensor_reduce(dot_terms[:, j, :], x2[:, j, :], row_b[:, 3, :], 1.0, 0.0,
                                                ALU.mult, ALU.add, dot2[:, j:j + 1])
                if j == TT - 1:
                    last.then_inc(x2_read, 1)

            def residual_stats(t):
                dve.wait_ge(x2_read, t + 1)
                dve.tensor_copy(dots[:, bass.ds(2 * t, TT)], dot2[:, :])
                dve.bn_aggr(mv2[:, 0, :], st6b[:, 0, :])
                dve.bn_aggr(mv2[:, 1, :], st6b[:, 1, :]).then_inc(mv2_ready, 1)
                dve.wait_ge(mv2_ready, t + 1)
                dve.tensor_copy(mean2[:, bass.ds(2 * t, TT)], mv2[:, :, 0:1].rearrange("p j o -> p (j o)")
                                ).then_inc(x2_stats, 1)

            def step(t, p, th, more=True, first=False):
                f, n = t + 1, t + 2
                mask_and_min(t, range(2, 4), p)
                probT_even(t, 0)
                mask_and_min(t, range(4, 6), p)
                square_sums_lat(f)
                mask_and_min(t, (6, 7), p)
                if more:
                    moments(n, p, th)
                probT_even(t, 2)
                square_sums_ctx(f)
                scale_lat(f)
                probT_even(t, 4)
                normalise_out(t, 0)
                if more:
                    normalise(n, p)
                latent_values(f, 1 - p)
                if not first:
                    residual_terms(t - 1, 0)
                probT_even(t, 6)
                if not first:
                    residual_terms(t - 1, 1)
                    residual_stats(t - 1)
                if more:
                    lat_high(n)
                normalise_out(t, 1)
                qT_low(f)
                oT_low(t, kind_bank["oT"])
                kT_low(f, 0)
                kT_low(f, 1)
                if more:
                    ctx_high(n)
                residual(t, kind_bank["y"])
                mask_and_min(f, (0, 1), 1 - p)

            moments(0, 0, 0)
            dve.wait_ge(vecs_in, 16)
            dve.tensor_tensor(neg_gqk[:, :], vk[:, 4:5], vk[:, 5:6], ALU.mult).then_inc(setup_v, 1)
            dve.wait_ge(setup_v, 1)
            dve.tensor_scalar(neg_gqk[:, :], neg_gqk[:, :], -float(DH) ** -0.5, None, ALU.mult).then_inc(setup_v, 1)
            normalise(0, 0, first=True)
            dve.wait_ge(wlat_hi_s, 1)
            dve.tensor_sub(wlat_lo[:, :, :], wlat_raw, wlat_hi[:, :, :].bitcast(F32)).then_inc(wlat_lo_s, 1)
            lat_high(0)
            ctx_high(0)
            dve.wait_ge(wctx_hi_s, 1)
            dve.tensor_sub(wctx_lo[:, :, :], wctx_raw, wctx_hi[:, :, :].bitcast(F32)).then_inc(wctx_lo_s, 1)
            moments(1, 1, 0)
            normalise(1, 1)
            square_sums_lat(0)
            latent_values(0, 0)
            square_sums_ctx(0)
            scale_lat(0)
            lat_high(1)
            ctx_high(1)
            dve.wait_ge(setup_v, 2)
            qT_low(0)
            for c in range(2):
                kT_low(0, c)
            dve.wait_ge(wo_hi_s, 1)
            dve.tensor_sub(wo_lo[:, :, :], wo_raw, wo_hi[:, :, :].bitcast(F32)).then_inc(wo_lo_s, 1)
            dve.wait_ge(rows_in, 16)
            dve.tensor_reduce(rt_sum[:, :], row_b[:, 3, :], AX_X, ALU.add).then_inc(setup_v, 1)
            mask_and_min(0, (0, 1), 0)
            step(0, 0, 1, first=True)
            step(1, 1, 1)
            with dve.Fori(1, (B - 2) // 2) as i:
                step(2 * i, 0, i + 1)
                step(2 * i + 1, 1, i + 1)
            step(B - 2, 0, None, more=False)
            mask_and_min(B - 1, range(2, 4), 1)
            probT_even(B - 1, 0)
            mask_and_min(B - 1, range(4, 8), 1)

            def z_tiles(g):
                for j in range(4):
                    last = dve.tensor_scalar(z[:, j, :], x_all[:, bass.ds(4 * g + j, 1), :].rearrange("p a d -> p (a d)"),
                                             mean2[:, bass.ds(4 * g + j, 1)], zs_col(g, j), ALU.subtract, ALU.mult)
                last.then_inc(z_ready, 1)

            def zs_col(g, j):
                return zr[:, bass.ds(2 * g + j // TT, 1), 1, j % TT:j % TT + 1].rearrange("p b o -> p (b o)")

            def zT_low(g, kts=(0, 1), first=False):
                for kt in kts:
                    dve.wait_ge(zT_hi_s, 2 * g + kt + 1)
                    src = bank[1 + kt] if first else bank[7]
                    dve.tensor_tensor(zT_lo[:, kt, :], src[:, :], zT_hi[:, kt, :].bitcast(F32), ALU.subtract
                                      ).then_inc(zT_lo_s, 1)

            def h_low(g, m):
                dve.wait_ge(h_hi_s, HT * g + m + 1)
                dve.tensor_tensor(h_lo[m % 3][:, :], h_raw[m % 3], h_hi[m % 3][:, :].bitcast(F32), ALU.subtract
                                  ).then_inc(h_lo_s, 1)

            def sums_out(g, heavy):
                dve.wait_ge(h_used, HT * (g + 1))
                dve.wait_ge(x_biased, g + 1)
                for j in range(4):
                    xt = x_all[:, bass.ds(4 * g + j, 1), :].rearrange("p a d -> p (a d)")
                    dve.tensor_tensor(xt, bank[j][:, 0:D], xt, ALU.add)
                    last = dve.tensor_tensor(heavy[:, j, :], bank[j][:, D:2 * D], row_b[:, 2, :], ALU.add)
                last.then_inc(acc_sb, 1)

            def final(g, heavy):
                dve.wait_ge(acc_sb, g + 2)
                for j in range(4):
                    xt = x_all[:, bass.ds(4 * g + j, 1), :].rearrange("p a d -> p (a d)")
                    last = dve.scalar_tensor_tensor(xt, heavy[:, j, :], sel[:, j % TT, bass.ds(2 * g + j // TT, 1)], xt,
                                                    ALU.mult, ALU.add)
                last.then_inc(fin, 1)

            def descent(lo, hi):
                for it in range(lo, hi):
                    dve.wait_ge(c_ready, it + 1)
                    dve.tensor_scalar(m16[:, :], e16[:, :], cc[:, 0:1], None, ALU.min, ALU.add, accum_out=cc[:, 2:3]
                                      ).then_inc(c_sum, 1)
                    dve.wait_ge(c_sum, it + 1)
                    dve.tensor_scalar(cc[:, 0:1], cc[:, 2:3], 1.0 / N, 1e-37, ALU.mult, ALU.max).then_inc(c_ready, 1)

            def multiplier():
                dve.wait_ge(c_ready, ITERS)
                dve.reciprocal(cc[:, 3:4], cc[:, 0:1]).then_inc(c_ready, 1)
                dve.wait_ge(c_ready, ITERS + 1)
                dve.tensor_scalar(m16[:, :], e16[:, :], cc[:, 3:4], 1.0, ALU.mult, ALU.min).then_inc(c_ready, 1)
                dve.wait_ge(c_ready, ITERS + 2)
                dve.tensor_scalar(s16[:, :], m16[:, :], -1.0, 1.0, ALU.mult, ALU.add).then_inc(c_ready, 1)
                dve.wait_ge(c_ready, ITERS + 3)
                dve.tensor_tensor(s16[:, :], s16[:, :], m16[:, :], ALU.add).then_inc(sel16_ready, 1)

            def score_tokens():
                dve.wait_ge(x2_stats, B)
                dve.tensor_scalar(sm[:, :], mean2[:, :], rt_sum[:, 0:1], None, ALU.mult).then_inc(descent_v, 1)
                dve.wait_ge(descent_v, 1)
                dve.tensor_tensor(sm[:, :], dots[:, :], sm[:, :], ALU.subtract).then_inc(descent_v, 1)
                dve.wait_ge(descent_v, 2)
                dve.wait_ge(zr_ready, B)
                dve.tensor_tensor(s_tok[:, :].rearrange("p (b j) -> p b j", j=TT),
                                  sm[:, :].rearrange("p (b j) -> p b j", j=TT),
                                  zr[:, :, 0, :], ALU.mult).then_inc(s_ready, 1)

            def score_exponents():
                dve.wait_ge(s16_ps, 1)
                dve.tensor_scalar(e16[:, :], bank[7][0:B, 0:N], 0.0, None, ALU.min).then_inc(s16_read, 1)
                dve.wait_ge(s16_read, 1)
                dve.tensor_reduce(cc[:, 1:2], e16[:, :], AX_X, ALU.max).then_inc(descent_v, 1)
                dve.wait_ge(descent_v, 3)
                dve.tensor_scalar(e16[:, :], e16[:, :], cc[:, 1:2], None, ALU.subtract).then_inc(e_ready, 1)

            SLOTS = {(g, m): i for i, (g, m) in enumerate([(0, m) for m in range(5, HT)]
                                                          + [(g, m) for g in (1, 2) for m in range(HT)])}

            def descend_in(g, m):
                i = SLOTS[g, m]
                descent((ITERS - 1) * i // len(SLOTS), (ITERS - 1) * (i + 1) // len(SLOTS))

            def last_tile(j):
                return x_all[:, TILES - 4 + j, :], sel[:, j % TT, B - TT + j // TT:B - TT + j // TT + 1]

            def last_bias():
                dve.wait_ge(x_biased, PAIRS)
                for j in range(4):
                    xt, factor = last_tile(j)
                    last = dve.scalar_tensor_tensor(xt, row_b[:, 2, :], factor, xt, ALU.mult, ALU.add)
                last.then_inc(last_s, 1)

            def last_light(j):
                dve.wait_ge(h_used, HT * PAIRS + j)
                xt, _ = last_tile(j)
                dve.tensor_tensor(xt, bank[j][:, 0:D], xt, ALU.add).then_inc(last_s, 1)

            def last_heavy(j):
                dve.wait_ge(last_s, j + 2)
                xt, factor = last_tile(j)
                last = dve.scalar_tensor_tensor(xt, bank[j][:, D:2 * D], factor, xt, ALU.mult, ALU.add)
                if j % TT == TT - 1:
                    last.then_inc(fin, 1)

            def selection_out():
                dve.wait_ge(sel_ps, 1)
                dve.tensor_copy(sel[:, :, :].rearrange("p j b -> p (j b)"), bank[7][:, 0:TT * B]).then_inc(sel_ready, 1)
                dve.wait_ge(sel_ready, 1)

            def ffn(g, heavy, more=True, descend=False, select=False, finish=()):
                for m in range(HT):
                    h_low(g, m)
                    if m == 2 and more:
                        z_tiles(g + 1)
                    if select and m == 2:
                        selection_out()
                    if 3 <= m < 3 + len(finish):
                        final(*finish[m - 3])
                    if more and m == HT - 1:
                        zT_low(g + 1, (0,))
                    if descend:
                        descend_in(g, m)
                    if not more and m == 5:
                        last_bias()
                if more:
                    zT_low(g + 1, (1,))
                    sums_out(g, heavy)

            probT_even(B - 1, 2)
            dve.wait_ge(x2_kept, TT)
            dve.wait_ge(zr_ready, TT)
            z_tiles(0)
            dve.wait_ge(zr_ready, B - 2)
            residual_terms(B - 2, 0)
            probT_even(B - 1, 4)
            normalise_out(B - 1, 0)
            residual_terms(B - 2, 1)
            residual_stats(B - 2)
            probT_even(B - 1, 6)
            zT_low(0, first=True)
            normalise_out(B - 1, 1)
            oT_low(B - 1, bank[0])
            h_low(0, 0)
            h_low(0, 1)
            dve.wait_ge(zr_ready, B - 1)
            residual(B - 1, bank[2])
            for j in range(TT):
                residual_terms(B - 1, j)
            residual_stats(B - 1)
            h_low(0, 2)
            score_tokens()
            dve.wait_ge(x2_kept, B)
            z_tiles(1)
            h_low(0, 3)
            score_exponents()
            h_low(0, 4)
            dve.wait_ge(exp_ready, 1)
            for m in range(5, HT):
                h_low(0, m)
                if m == HT - 1:
                    zT_low(1, (0,))
                descend_in(0, m)
            zT_low(1, (1,))
            sums_out(0, hv[0])
            for g in (1, 2):
                ffn(g, hv[g], descend=True)
            multiplier()
            ffn(3, hv[2], select=True, finish=((0, hv[0]), (1, hv[1]), (2, hv[2])))
            with dve.Fori(4, PAIRS - 1) as g:
                ffn(g, hv[2], finish=((g - 1, hv[2]),))
            ffn(PAIRS - 1, hv[2], more=False, finish=((PAIRS - 2, hv[2]),))
            dve.wait_ge(last_s, 1)
            last_light(0)
            for j in range(1, 4):
                last_light(j)
                last_heavy(j - 1)
            last_heavy(3)

        @block.scalar
        def _(act):
            act.dma_start(vecs_sb[:, :], vecs).then_inc(vecs_in, 16)
            act.dma_start(row_b[:, :, :], rows.rearrange("(o r) d -> o r d", o=1).broadcast_to([P, 4, D])
                          ).then_inc(rows_in, 16)

            def front_out(f, first=False):
                act.wait_ge(ps["lnT"], f + 1)
                if not first:
                    act.wait_ge(lnT_lo_ready, f)
                for k in range(2):
                    last = act.activation(lnT[:, k, :], kind_bank["lnT"][:, k * N:(k + 1) * N], ACT.Identity,
                                          bias=vk[:, 2 + k:3 + k], scale=vk[:, k:k + 1])
                last.then_inc(rd["lnT"], 1)
                act.wait_ge(ps["cT"], f + 1)
                if not first:
                    act.wait_ge(cT_lo_ready, f)
                    act.wait_ge(cT_stacked, f)
                for k in range(2):
                    last = act.activation(cT[:, k, :], kind_bank["cT"][:, k * N:(k + 1) * N], ACT.Identity,
                                          bias=vc[:, 2 + k:3 + k], scale=vc[:, k:k + 1])
                last.then_inc(rd["cT"], 1)

            def qk_out(f, j, first=False):
                act.wait_ge(ps[f"qk{j}"], f + 1)
                if j == 0 and not first:
                    act.wait_ge(ps["kT1"], f)
                    act.wait_ge(ss_ctx, f)
                act.copy(qk[:, j, :], kind_bank[f"qk{j}"][:, :])
                act.activation(sq[:, 2 * j:2 * j + 2, :].rearrange("p a d -> p (a d)"), kind_bank[f"qk{j}"][:, :],
                               ACT.Square).then_inc(rd[f"qk{j}"], 1)

            def kv_out(f, fp):
                for j in range(TT):
                    act.wait_ge(ps[f"kv{j}"], f + 1)
                    act.copy(kc[:, j, :], kind_bank[f"kv{j}"][:, 0:D])
                    act.activation(sq[:, 4 + j, :], kind_bank[f"kv{j}"][:, 0:D], ACT.Square)
                    act.copy(v_aug[fp][:, TT + j, :, 0:DH],
                             kind_bank[f"kv{j}"][:, D:2 * D].rearrange("p (h d) -> p h d", h=HEADS)
                             ).then_inc(rd[f"kv{j}"], 1)

            def qT_high(f):
                act.wait_ge(ps["qT"], f + 1)
                act.activation(qT_hi.rearrange("p c n -> p (c n)"), kind_bank["qT"][:, :], ACT.Identity,
                               scale=neg_gqk[:, 0:1]).then_inc(hi_s["qT"], 1)

            def kT_high(f, c):
                act.wait_ge(ps[f"kT{c}"], f + 1)
                act.copy(kT_hi[:, c, :], kind_bank[f"kT{c}"][:, :]).then_inc(hi_s[f"kT{c}"], 1)

            def oT_high(t, src):
                act.wait_ge(ps["oT"], t + 1)
                act.copy(oT_hi[:, :, :].rearrange("p c n -> p (c n)"), src[:, :]).then_inc(hi_s["oT"], 1)

            def keep_x2(t):
                act.wait_ge(rd["y"], t + 2)
                act.copy(x_all[:, bass.ds(2 * t, TT), :], x2[:, :, :]).then_inc(x2_kept, 1)

            def exponentials(t, units):
                for u in units:
                    act.wait_ge(s_masked, 8 * t + u + 3)
                    act.activation(prob[:, u, :], prob[:, u, :], ACT.Exp, bias=mn[:, u:u + 1], scale=-1.0
                                   ).then_inc(p_ready, 1)

            def probT_odd(t, u):
                act.wait_ge(pt_ps, 8 * t + u + 1)
                if u >= 4:
                    act.wait_ge(pv_done, 8 * t + u - 3)
                act.copy(probT[:, u % 4, :, :].rearrange("p k q -> p (k q)"), pt_bank[1][:, :]).then_inc(pt_odd, 1)

            def prepare_weights(part):
                if part < 2:
                    if part == 0:
                        act.wait_ge(w1_in, 16)
                    for c, g in ((slice(0, HID_L), part), (slice(HID_L, HT * P), 2 + part)):
                        last = act.activation(w1_raw[:, part, c], w1_raw[:, part, c], ACT.Identity, scale=vh[:, g:g + 1])
                    last.then_inc(w1_scaled, 1)
                elif part < 4:
                    k = part - 2
                    act.wait_ge(w1_scaled, k + 1)
                    act.copy(w1_hi[:, k, :], w1_raw[:, k, :]).then_inc(w_hi_s, 1)
                else:
                    if part == 4:
                        act.wait_ge(w2_in, 16)
                    m = slice(HT * (part - 4) // 4, HT * (part - 3) // 4)
                    act.copy(w2_hi[:, m, :], w2_raw[:, m, :]).then_inc(w_hi_s, 1)

            act.wait_ge(vecs_in, 16)
            act.copy(cred[:, 0:1], vk[:, 0:1]).then_inc(pt_odd, 1)
            act.copy(cred[:, 1:2], vk[:, 0:1]).then_inc(gelu_done, 3)
            act.wait_ge(wlat_in, 16)
            act.copy(wlat_hi[:, :, :], wlat_raw).then_inc(wlat_hi_s, 1)
            front_out(0, first=True)
            act.wait_ge(wctx_in, 16)
            act.copy(wctx_hi[:, :, :], wctx_raw).then_inc(wctx_hi_s, 1)
            for j in range(TT):
                qk_out(0, j, first=True)
            kv_out(0, 0)
            front_out(1)
            act.wait_ge(setup_v, 2)
            qT_high(0)
            kT_high(0, 0)
            kT_high(0, 1)
            act.wait_ge(wo_in, 16)
            act.copy(wo_hi[:, :, :], wo_raw).then_inc(wo_hi_s, 1)
            qk_out(1, 0)

            def step(t, p, more=True, weights=None):
                f, n = t + 1, t + 2
                exponentials(t, (0, 1))
                qk_out(f, 1)
                exponentials(t, (2, 3))
                exponentials(t, (4, 5, 6, 7))
                for u in (1, 3, 5, 7):
                    probT_odd(t, u)
                    if u == 1:
                        kv_out(f, 1 - p)
                    if weights is not None:
                        prepare_weights(weights + u // 2)
                if more:
                    front_out(n)
                qT_high(f)
                kT_high(f, 0)
                oT_high(t, kind_bank["oT"])
                kT_high(f, 1)
                if more:
                    qk_out(n, 0)
                keep_x2(t)

            step(0, 0, weights=0)
            step(1, 1, weights=4)
            with act.Fori(1, (B - 2) // 2) as i:
                step(2 * i, 0)
                step(2 * i + 1, 1)
            step(B - 2, 0, more=False)
            exponentials(B - 1, range(6))
            probT_odd(B - 1, 1)
            exponentials(B - 1, (6, 7))

            def zT_high(g, first=False):
                for kt in range(2):
                    src = bank[1 + kt] if first else bank[7]
                    act.wait_ge(zT_ps, 2 * g + kt + 1)
                    act.copy(zT_hi[:, kt, :], src[:, :]).then_inc(zT_hi_s, 1)

            def gelu(g, m, early):
                act.wait_ge(h_ps, HT * g + m + 1)
                if not early:
                    act.wait_ge(h_lo_s, HT * g + m - 2)
                act.activation(h_raw[m % 3], bank[4 + m % 3][:, :], ACT.Gelu, bias=vh[:, 4 + m:5 + m]
                               ).then_inc(gelu_done, 1)
                act.wait_ge(gelu_done, HT * g + m + 4)
                if not early:
                    act.wait_ge(h_used, HT * g + m - 2)
                act.copy(h_hi[m % 3][:, :], h_raw[m % 3]).then_inc(h_hi_s, 1)

            def ffn(g, more=True):
                for m in range(HT):
                    gelu(g, m, False)
                if more:
                    zT_high(g + 1)

            probT_odd(B - 1, 3)
            zT_high(0, first=True)
            probT_odd(B - 1, 5)
            probT_odd(B - 1, 7)
            gelu(0, 0, True)
            oT_high(B - 1, bank[0])
            gelu(0, 1, True)
            keep_x2(B - 1)
            for m in range(2, 6):
                gelu(0, m, m < 3)
            act.wait_ge(e_ready, 1)
            act.activation(e16[:, :], e16[:, :], ACT.Exp).then_inc(exp_ready, 1)
            for m in range(6, HT):
                gelu(0, m, False)
            zT_high(1)
            with act.Fori(1, PAIRS - 1) as g:
                ffn(g)
            ffn(PAIRS - 1, more=False)

        @block.gpsimd
        def _(pool):
            pool.memset(neg_half[:, :], -0.5).then_inc(setup_p, 1)
            pool.memset(maskb[0][:, :], 0.0).then_inc(setup_p, 1)
            pool.memset(maskb[1][:, :], 0.0).then_inc(setup_p, 1)
            pool.wait_ge(setup_p, 3)

            def inverse_std(b):
                pool.wait_ge(mv_ready, b + 1)
                pool.sem_inc(turn_p)
                v = mv[:, :, 1:2].rearrange("p t o -> p (t o)")
                pool.tensor_scalar(rstd[:, 0:TT], v[:, 0:TT], 1.0 + LN_EPS, LN_EPS * LN_EPS, ALU.mult, ALU.add)
                pool.tensor_scalar(rstd[:, TT:4], v[:, TT:4], 1.0, LN_EPS, ALU.mult, ALU.add).then_inc(pool_step, 1)
                pool.wait_ge(pool_step, b + 1)
                pool.tensor_tensor(rstd[:, :], rstd[:, :], neg_half[:, 0:4], ALU.pow).then_inc(rstd_ready, 1)

            def low_parts(f):
                pool.wait_ge(lnT_hi_ready, f + 1)
                pool.tensor_tensor(lnT_lo[:, :, :], lnT[:, :, :], lnT_hi[:, :, :].bitcast(F32), ALU.subtract
                                   ).then_inc(lnT_lo_ready, 1)
                pool.wait_ge(cT_hi_ready, f + 1)
                pool.tensor_tensor(cT_lo[:, :], cT[:, 0, :], cT_hi[:, 0, :].bitcast(F32), ALU.subtract
                                   ).then_inc(cT_lo_ready, 1)

            def mask_bias(b, p):
                pool.tensor_copy(maskb[p][:, N:KEYS], mask_all[:, bass.ds(b * N, N)]).then_inc(pool_step2, 1)
                pool.wait_ge(pool_step2, b + 1)
                pool.sem_inc(turn_p)
                pool.tensor_scalar(maskb[p][:, N:KEYS], maskb[p][:, N:KEYS], -1.0, -BIG, ALU.add, ALU.mult
                                   ).then_inc(mask_ready, 1)

            def add_bo(b):
                pool.wait_ge(ln_ready, b + 1)
                xt = x_all[:, bass.ds(2 * b, TT), :]
                pool.tensor_tensor(xt, xt, row_b[:, 0:1, :].broadcast_to([P, TT, D]), ALU.add).then_inc(xbo_ready, 1)

            def inverse_norms(f, lat):
                c = slice(0, 16) if lat else slice(16, 24)
                pool.wait_ge(ss_lat if lat else ss_ctx, f + 1)
                pool.sem_inc(turn_p)
                pool.tensor_scalar(ss[:, c], ss[:, c], 1.0 / DH, 1e-16, ALU.mult, ALU.max).then_inc(norm_step, 1)
                pool.wait_ge(norm_step, 2 * f + (1 if lat else 2))
                pool.tensor_tensor(rr[:, c], ss[:, c], neg_half[:, c], ALU.pow).then_inc(rr_lat if lat else rr_ctx, 1)

            def scale_ctx(f):
                pool.wait_ge(rr_ctx, f + 1)
                v = kc[:, :, :].rearrange("p j (h d) -> p (j h) d", d=DH)
                pool.tensor_tensor(v, v, rr[:, 16:24].rearrange("p (h o) -> p h o", o=1).broadcast_to([P, 8, DH]),
                                   ALU.mult).then_inc(ctx_scaled, 1)

            def second_scales(t):
                pool.wait_ge(mv2_ready, t + 1)
                pool.sem_inc(turn_p)
                v = mv2[:, :, 1:2].rearrange("p j o -> p (j o)")
                pool.tensor_scalar(vtmp[:, 0, :], v, 1.0, LN_EPS, ALU.mult, ALU.add)
                pool.tensor_scalar(vtmp[:, 1, :], v, 1.0, 1e-24 / D * LN_EPS, ALU.mult, ALU.max).then_inc(zr_step, 1)
                pool.wait_ge(zr_step, t + 1)
                pool.tensor_tensor(zr[:, bass.ds(t, 1), :, :].rearrange("p b k j -> p (b k j)"),
                                   vtmp[:, :, :].rearrange("p k j -> p (k j)"), neg_half[:, 0:4], ALU.pow
                                   ).then_inc(zr_ready, 1)

            inverse_std(0)
            low_parts(0)
            inverse_std(1)
            inverse_norms(0, True)
            inverse_norms(0, False)
            scale_ctx(0)
            low_parts(1)
            pool.wait_ge(mask_in, 16)
            mask_bias(0, 0)
            pool.wait_ge(rows_in, 16)
            add_bo(0)
            mask_bias(1, 1)
            add_bo(1)

            def w1_low():
                for k in range(2):
                    pool.wait_ge(w_hi_s, k + 1)
                    pool.tensor_tensor(w1_lo[:, k, :], w1_raw[:, k, :], w1_hi[:, k, :].bitcast(F32), ALU.subtract
                                       ).then_inc(w_lo_s, 1)

            def w2_low():
                for c in range(4):
                    pool.wait_ge(w_hi_s, c + 3)
                    m = slice(HT * c // 4, HT * (c + 1) // 4)
                    pool.tensor_tensor(w2_lo[:, m, :], w2_raw[:, m, :], w2_hi[:, m, :].bitcast(F32), ALU.subtract
                                       ).then_inc(w_lo_s, 1)

            def step(t, p, more=True, weights=None, first=False):
                f, n = t + 1, t + 2
                inverse_norms(f, True)
                if more:
                    inverse_std(n)
                inverse_norms(f, False)
                scale_ctx(f)
                if more:
                    low_parts(n)
                    mask_bias(n, p)
                    add_bo(n)
                if weights is not None:
                    weights()
                if not first:
                    second_scales(t - 1)

            step(0, 0, weights=w1_low, first=True)
            step(1, 1, weights=w2_low)
            with pool.Fori(1, (B - 2) // 2) as i:
                step(2 * i, 0)
                step(2 * i + 1, 1)
            step(B - 2, 0, more=False)
            second_scales(B - 2)
            second_scales(B - 1)

            def bias_x(g):
                pool.wait_ge(z_ready, g + 1)
                xt = x_all[:, bass.ds(4 * g, 4), :]
                pool.tensor_tensor(xt, xt, row_b[:, 1:2, :].broadcast_to([P, 4, D]), ALU.add).then_inc(x_biased, 1)

            with pool.Fori(0, PAIRS) as g:
                bias_x(g)


def kernel(**inputs):
    import concourse.bacc as bacc
    from concourse.bass_utils import run_bass_kernel_spmd

    def get(name):
        return np.asarray(inputs[name])

    def cols(v):
        return np.ascontiguousarray(v.reshape(-1, P).T)

    def pre(name):
        return get("L0_ffn_" + name)

    w_lat = np.concatenate([get("L0_xattn_Wq").T, get("L0_xattn_Wlkv").T], axis=1)
    w_ctx = get("L0_xattn_Wkv").T
    w_ctx = np.concatenate([w_ctx, w_ctx[P:DC]], axis=0)

    def ctx_vec(v):
        return cols(np.concatenate([v, v[P:DC]]))

    def head_vec(v):
        return np.concatenate([v, v])[:, None]

    arrays = {
        "x": get("x"),
        "ctx_in": get("ctx_768"),
        "mask": get("mask_BxS2_bk0"),
        "w_lat": w_lat,
        "w_ctx": w_ctx,
        "w_o": get("L0_xattn_Wo").T,
        "w1": np.concatenate([pre("light_w1"), pre("heavy_w1")], axis=1),
        "w2": np.concatenate([pre("light_w2"), pre("heavy_w2")], axis=0),
        "vecs": np.concatenate([
            cols(get("L0_xattn_ln_l_g")), cols(get("L0_xattn_ln_l_b")),
            head_vec(get("L0_xattn_qn_g")), head_vec(get("L0_xattn_kn_g")),
            ctx_vec(get("L0_xattn_ln_x_g")), ctx_vec(get("L0_xattn_ln_x_b")),
            cols(pre("light_gamma")), cols(pre("heavy_gamma")), cols(pre("light_b1")), cols(pre("heavy_b1")),
            np.eye(P, dtype=np.float32)], axis=1),
        "rows": np.stack([get("L0_xattn_bo"), pre("light_b2"), pre("heavy_b2"), pre("routing_token")]),
    }
    arrays = {k: np.ascontiguousarray(v) for k, v in arrays.items()}
    nc = bacc.Bacc("TRN2", target_bir_lowering=False, num_devices=1)
    aps = [nc.dram_tensor("in_" + k, v.shape, mybir.dt.from_np(v.dtype), kind="ExternalInput").ap()
           for k, v in arrays.items()]
    out = nc.dram_tensor("out_0", (B, N, D), F32, kind="ExternalOutput").ap()
    build(nc, *aps, out)
    r = run_bass_kernel_spmd(nc, [{"in_" + k: v for k, v in arrays.items()}], core_ids=[0])
    return r.results[0]["out_0"]
```
